# Optimizing a Trainium2 kernel written in Bass

```python
import numpy as np
import jax
import jax.numpy as jnp

def _softmax(x, axis=-1):
    return jax.nn.softmax(x, axis=axis)

def _gelu(x):
    return jax.nn.gelu(x, approximate=True)

def _silu(x):
    return jax.nn.silu(x)

def _sigmoid(x):
    return jax.nn.sigmoid(x)

def _layernorm(x, axis=-1, eps=1e-05):
    m = jnp.mean(x, axis=axis, keepdims=True)
    v = jnp.var(x, axis=axis, keepdims=True)
    return (x - m) / jnp.sqrt(v + eps)

def _scatter_add(tgt, idx, src, axis=0):
    return tgt.at[idx].add(src)

def _segment_sum(src, seg, n):
    return jax.ops.segment_sum(src, seg, n)
kernel_name = 'mk_flamingo_gated_d1_seqx_r2_d109e3'

def setup_inputs(seed: int=0):
    np.random.seed(seed)
    _w = jnp.asarray

    def _rec_inputs():
        import jax
        import jax.numpy as jnp
        _rk = jax.random.key(seed)
        x = -0.000125 + 0.9999 * jax.random.normal(jax.random.fold_in(_rk, 1), (8, 512, 2048), jnp.float32)
        _lenS = 512 - jax.random.randint(jax.random.fold_in(_rk, 7), (8,), 0, max(1, 512 // 4) + 1, jnp.int32)
        _lenS2 = 512 - jax.random.randint(jax.random.fold_in(_rk, 8), (8,), 0, max(1, 512 // 4) + 1, jnp.int32)
        _ctx_4096P = jax.random.normal(jax.random.fold_in(_rk, 11), (8, 16, 2048), jnp.float32)
        _ctx_4096c = jax.random.dirichlet(jax.random.fold_in(_rk, 511), 0.3 * jnp.ones((16,), jnp.float32), (8, 512))
        _ctx_4096t = jnp.einsum('bsk,bkd->bsd', _ctx_4096c, _ctx_4096P)
        _ctx_4096t = _ctx_4096t * jax.lax.rsqrt(jnp.mean(jnp.square(_ctx_4096t)) + 1e-12) * 0.953939
        ctx_4096 = -1.52775e-05 + 0.999936 * (_ctx_4096t + 0.3 * jax.random.normal(jax.random.fold_in(_rk, 611), (8, 512, 2048), jnp.float32))
        _validS = jnp.arange(512)[None, :] < _lenS[:, None]
        _validS2 = jnp.arange(512)[None, :] < _lenS2[:, None]
        _causal = jnp.tril(jnp.ones((512, 512), dtype=bool))
        mask_Bx1x4096_ff1 = jnp.where(jnp.ones((8, 1, 2048), dtype=bool), 1.0, 0.0).astype(jnp.float32)
        _g = jax.random.normal(jax.random.fold_in(_rk, 9001), (2, 1), jnp.float32)
        _g = jnp.sign(_g) * jnp.maximum(jnp.abs(_g), 1.0) + (_g == 0) * 1.0
        g_xattn = _g[0]
        g_ffn = _g[1]
        return (x, ctx_4096, mask_Bx1x4096_ff1, g_xattn, g_ffn)
    x, ctx_4096, mask_Bx1x4096_ff1, g_xattn, g_ffn = _rec_inputs()

    def _L0_xattn_setup():
        import jax, jax.numpy as jnp
        import numpy as np
        W = 128
        H = 8
        D = 512
        DK = D // 2

        def _to_patches(x):
            b, d, s = x.shape
            np_ = s // W
            return x.reshape(b, d, np_, W).transpose(0, 2, 1, 3).reshape(b * np_, d, W)
        key = jax.random.key(seed)
        ks = jax.random.split(key, 10)
        B, S = (8, 2048)
        qk = jax.random.normal(ks[0], (B, D, S), dtype=jnp.float32)
        v = jax.random.normal(ks[1], (B, D, S), dtype=jnp.float32)
        masks = jnp.ones((B, 1, S), dtype=jnp.float32)
        sc = 1.0 / np.sqrt(D)
        Wq = jax.random.normal(ks[2], (DK, D), dtype=jnp.float32) * sc
        bq = jnp.zeros((DK,), dtype=jnp.float32)
        Wk = jax.random.normal(ks[3], (DK, D), dtype=jnp.float32) * sc
        bk = jnp.zeros((DK,), dtype=jnp.float32)
        Wv = jax.random.normal(ks[4], (DK, D), dtype=jnp.float32) * sc
        bv = jnp.zeros((DK,), dtype=jnp.float32)
        Wo = jax.random.normal(ks[5], (D, DK), dtype=jnp.float32) * (1.0 / np.sqrt(DK))
        bo = jnp.zeros((D,), dtype=jnp.float32)
        return dict(qk=qk, v=v, masks=masks, Wq=Wq, bq=bq, Wk=Wk, bk=bk, Wv=Wv, bv=bv, Wo=Wo, bo=bo)
    _L0_xattn_all = _L0_xattn_setup()
    _L0_xattn_in = {k: v for k, v in _L0_xattn_all.items() if k in ('Wq', 'bq', 'Wk', 'bk', 'Wv', 'bv', 'Wo', 'bo')}
    del _L0_xattn_all

    def _L0_ffn_setup():
        import jax, jax.numpy as jnp
        import numpy as np
        N_STREAMS = 4
        DIM = 512
        SINKHORN_ITERS = 50
        SINKHORN_TAU = 0.1
        RMS_EPS = 1.1920929e-07

        def sinkhorn_log(logits, num_iters=SINKHORN_ITERS, tau=SINKHORN_TAU):
            Z = logits / tau
            u0 = jnp.zeros(Z.shape[:-1], Z.dtype)
            v0 = jnp.zeros_like(u0)

            def step(carry, _):
                u, v = carry
                u = -jax.nn.logsumexp(Z + v[..., None, :], axis=-1)
                v = -jax.nn.logsumexp(Z + u[..., :, None], axis=-2)
                return ((u, v), None)
            (u, v), _ = jax.lax.scan(step, (u0, v0), None, length=num_iters)
            return jnp.exp(Z + u[..., :, None] + v[..., None, :])
        key = jax.random.key(seed)
        ks = jax.random.split(key, 6)
        B, T = (4, 1024)
        n, C = (N_STREAMS, DIM)
        wd = n * C
        x = jax.random.normal(ks[0], (B, T, wd), dtype=jnp.float32)
        W_res = 0.01 * jax.random.normal(ks[1], (n * n, wd), dtype=jnp.float32)
        W_pre = 0.01 * jax.random.normal(ks[2], (n, wd), dtype=jnp.float32)
        W_post = 0.01 * jax.random.normal(ks[3], (n, wd), dtype=jnp.float32)
        H_res_base = jnp.full((n, n), -0.5, dtype=jnp.float32)
        H_res_base = H_res_base.at[jnp.arange(n), jnp.arange(n)].set(0.0)
        H_pre_base = jnp.zeros((n,), dtype=jnp.float32).at[0].set(1.0)
        H_post_base = jnp.zeros((n,), dtype=jnp.float32)
        gate = jnp.array([5.0], dtype=jnp.float32)
        W_branch = 1.0 / np.sqrt(C) * jax.random.normal(ks[4], (C, C), dtype=jnp.float32)
        return {'x': x, 'W_res': W_res, 'W_pre': W_pre, 'W_post': W_post, 'H_res_base': H_res_base, 'H_pre_base': H_pre_base, 'H_post_base': H_post_base, 'gate': gate, 'W_branch': W_branch}
    _L0_ffn_all = _L0_ffn_setup()
    _L0_ffn_in = {k: v for k, v in _L0_ffn_all.items() if k in ('W_res', 'W_pre', 'W_post', 'H_res_base', 'H_pre_base', 'H_post_base', 'gate', 'W_branch')}
    del _L0_ffn_all
    return {'x': x, 'ctx_4096': ctx_4096, 'mask_Bx1x4096_ff1': mask_Bx1x4096_ff1, 'g_xattn': g_xattn, 'g_ffn': g_ffn, 'L0_xattn_Wq': _L0_xattn_in['Wq'], 'L0_xattn_bq': _L0_xattn_in['bq'], 'L0_xattn_Wk': _L0_xattn_in['Wk'], 'L0_xattn_bk': _L0_xattn_in['bk'], 'L0_xattn_Wv': _L0_xattn_in['Wv'], 'L0_xattn_bv': _L0_xattn_in['bv'], 'L0_xattn_Wo': _L0_xattn_in['Wo'], 'L0_xattn_bo': _L0_xattn_in['bo'], 'L0_ffn_W_res': _L0_ffn_in['W_res'], 'L0_ffn_W_pre': _L0_ffn_in['W_pre'], 'L0_ffn_W_post': _L0_ffn_in['W_post'], 'L0_ffn_H_res_base': _L0_ffn_in['H_res_base'], 'L0_ffn_H_pre_base': _L0_ffn_in['H_pre_base'], 'L0_ffn_H_post_base': _L0_ffn_in['H_post_base'], 'L0_ffn_gate': _L0_ffn_in['gate'], 'L0_ffn_W_branch': _L0_ffn_in['W_branch']}

def reference(x, ctx_4096, mask_Bx1x4096_ff1, g_xattn, g_ffn, L0_xattn_Wq, L0_xattn_bq, L0_xattn_Wk, L0_xattn_bk, L0_xattn_Wv, L0_xattn_bv, L0_xattn_Wo, L0_xattn_bo, L0_ffn_W_res, L0_ffn_W_pre, L0_ffn_W_post, L0_ffn_H_res_base, L0_ffn_H_pre_base, L0_ffn_H_post_base, L0_ffn_gate, L0_ffn_W_branch):
    import jax
    import jax.numpy as jnp

    def _L0_xattn_ref(qk, v, masks, Wq, bq, Wk, bk, Wv, bv, Wo, bo):
        import jax, jax.numpy as jnp
        import numpy as np
        W = 128
        H = 8
        D = 512
        DK = D // 2

        def _to_patches(x):
            b, d, s = x.shape
            np_ = s // W
            return x.reshape(b, d, np_, W).transpose(0, 2, 1, 3).reshape(b * np_, d, W)
        B, _, S = qk.shape
        np_ = S // W
        qp = _to_patches(qk)
        vp = _to_patches(v)
        mp = _to_patches(masks)
        q = jnp.einsum('ed,bdw->bew', Wq, qp) + bq[:, None]
        k = jnp.einsum('ed,bdw->bew', Wk, qp) + bk[:, None]
        val = jnp.einsum('ed,bdw->bew', Wv, vp) + bv[:, None]
        BN = q.shape[0]
        dh = DK // H
        qh = q.reshape(BN, H, dh, W)
        kh = k.reshape(BN, H, dh, W)
        vh = val.reshape(BN, H, dh, W)
        scores = jnp.einsum('bhdi,bhdj->bhij', qh, kh) / jnp.sqrt(jnp.asarray(dh, qh.dtype))
        scores = jnp.where(mp[:, :, None, :] > 0, scores, jnp.asarray(-1000000000.0, scores.dtype))
        attn = jax.nn.softmax(scores, axis=-1)
        o = jnp.einsum('bhij,bhdj->bhdi', attn, vh).reshape(BN, DK, W)
        o = jax.nn.gelu(o, approximate=False)
        out = jnp.einsum('de,bew->bdw', Wo, o) + bo[:, None]
        out = out.reshape(B, np_, D, W).transpose(0, 2, 1, 3).reshape(B, D, S)
        out = out * masks
        return out

    def _L0_ffn_ref(x, W_res, W_pre, W_post, H_res_base, H_pre_base, H_post_base, gate, W_branch):
        import jax, jax.numpy as jnp
        import numpy as np
        N_STREAMS = 4
        DIM = 512
        SINKHORN_ITERS = 50
        SINKHORN_TAU = 0.1
        RMS_EPS = 1.1920929e-07

        def sinkhorn_log(logits, num_iters=SINKHORN_ITERS, tau=SINKHORN_TAU):
            Z = logits / tau
            u0 = jnp.zeros(Z.shape[:-1], Z.dtype)
            v0 = jnp.zeros_like(u0)

            def step(carry, _):
                u, v = carry
                u = -jax.nn.logsumexp(Z + v[..., None, :], axis=-1)
                v = -jax.nn.logsumexp(Z + u[..., :, None], axis=-2)
                return ((u, v), None)
            (u, v), _ = jax.lax.scan(step, (u0, v0), None, length=num_iters)
            return jnp.exp(Z + u[..., :, None] + v[..., None, :])
        B, T, nC = x.shape
        n = N_STREAMS
        C = nC // n
        x_norm = x * jax.lax.rsqrt(jnp.mean(x * x, axis=-1, keepdims=True) + RMS_EPS)
        H_res_logits = (x_norm @ W_res.T).reshape(B, T, n, n) + H_res_base
        H_pre_logits = x_norm @ W_pre.T + H_pre_base
        H_post_logits = x_norm @ W_post.T + H_post_base
        H_res = sinkhorn_log(H_res_logits)
        H_pre = jax.nn.softmax(H_pre_logits, axis=-1)
        H_post = jax.nn.softmax(H_post_logits, axis=-1)
        g = jax.nn.sigmoid(gate)[0]
        I = jnp.eye(n, dtype=H_res.dtype)
        H_res = (1.0 - g) * I + g * H_res
        x_streams = x.reshape(B, T, n, C)
        x_pre = jnp.einsum('btnc,btn->btc', x_streams, H_pre)
        y = x_pre @ W_branch
        x_mixed = jnp.einsum('btij,btjc->btic', H_res, x_streams)
        y_distributed = jnp.einsum('btc,btn->btnc', y, H_post)
        return (x_mixed + y_distributed).reshape(B, T, nC)
    x = x + jnp.tanh(g_xattn[0]) * _L0_xattn_ref(_layernorm(x, axis=-1), ctx_4096, mask_Bx1x4096_ff1, L0_xattn_Wq, L0_xattn_bq, L0_xattn_Wk, L0_xattn_bk, L0_xattn_Wv, L0_xattn_bv, L0_xattn_Wo, L0_xattn_bo)
    x = x + jnp.tanh(g_ffn[0]) * _L0_ffn_ref(_layernorm(x, axis=-1), L0_ffn_W_res, L0_ffn_W_pre, L0_ffn_W_post, L0_ffn_H_res_base, L0_ffn_H_pre_base, L0_ffn_H_post_base, L0_ffn_gate, L0_ffn_W_branch)
    return x

_drawn_inputs = setup_inputs


def setup_inputs(seed=0):
    import zlib

    import numpy as np

    out = dict(_drawn_inputs(seed))
    spreads = {'L0_xattn_bq': (0.0, 0.8),
     'L0_xattn_bk': (0.0, 0.8),
     'L0_xattn_bv': (0.0, 0.1),
     'L0_xattn_bo': (0.0, 0.1),
     'L0_ffn_H_post_base': (0.0, 0.642)}
    factors = {}
    for name, (base, spread) in spreads.items():
        noise = np.random.default_rng([zlib.crc32(name.encode()), seed]).standard_normal(out[name].shape)
        drawn = base * np.exp(spread * noise) if base else spread * noise
        out[name] = jnp.asarray(drawn.astype(out[name].dtype))
    for name, factor in factors.items():
        out[name] = (out[name] * factor).astype(out[name].dtype)
    return out
```

```python
from contextlib import ExitStack

import concourse.bass as bass
from concourse import mybir

F32 = mybir.dt.float32
BF16 = mybir.dt.bfloat16
ALU = mybir.AluOpType
ACT = mybir.ActivationFunctionType
AX = mybir.AxisListType

P = 128
B, D, S = 8, 512, 2048
W = 128
HEADS, DH = 8, 32
E = HEADS * DH
DT = D // P
ET = E // P
HPT = P // DH
CH = 2 * W
NC = S // CH
WPC = CH // W
UNITS = S // W * ET
UPC = UNITS // NC
WO_COLS = 512
NW = S // WO_COLS
SCALE = float(DH) ** -0.5
NEG = -float(2 ** 30)
LN_EPS = 1e-5
RMS_EPS = 1.1920929e-07
N = 4
C = S // N
NL = 32
ITERS = 50
TAU = 0.1
SEG = 10

BD = 16 * 2 * HPT
PROJ = 3 * NC
USES = PROJ + DT * NW
SC = S // P
RETURNS = range(SEG, ITERS, SEG)
SMALL = 10 + 3 * len(RETURNS)
DVE_ATT = 6
DVE_FFN = 343


def bcast(ap, axis, n):
    ap = ap.unsqueeze(axis)
    shape = list(ap.shape)
    shape[axis] = n
    return ap.broadcast_to(shape)


class Chain:

    def __init__(self, eng, sem, per_batch):
        self.eng, self.sem, self.per, self.n, self.base = eng, sem, per_batch, 0, 0

    def start(self, b):
        self.n, self.base = 0, b * self.per

    def link(self, ins):
        self.n += 1
        ins.then_inc(self.sem, 1)
        self.eng.wait_ge(self.sem, self.base + self.n)

    def end(self):
        assert self.n == self.per, (self.n, self.per)


def program(nc, x, ctx4, mask_bc, mask_t, gates, wq_t, bq, wk_t, bk, wv_t, bv, wo_t, bo, wf_t, base,
            w_branch, ident, stack_i, eye4, out):
    with ExitStack() as ctx:
        def sb(name, shape, dt=F32):
            return ctx.enter_context(nc.sbuf_tensor(name, shape, dt))

        def ps(name):
            return ctx.enter_context(nc.psum_tensor(name, [P, 512], F32))

        def sem(name):
            return ctx.enter_context(nc.semaphore(name))

        xa = sb("xa", [P, DT, S])
        xb = sb("xb", [P, DT, S])
        ctx_sb = sb("ctx_sb", [P, 2, DT, CH])
        xn = sb("xn", [P, 2, DT, CH])
        q_sb = sb("q_sb", [P, 2, ET, CH])
        k_sb = sb("k_sb", [P, 2, ET, CH])
        q_bd = sb("q_bd", [P, 2, ET, WPC, HPT, W])
        k_bd = sb("k_bd", [P, 2, ET, WPC, HPT, W])
        v_t = sb("v_t", [P, 2, WPC, E])
        probs = sb("probs", [P, 2, HPT * W])
        o_sb = sb("o_sb", [P, ET, S])
        maskbc = sb("maskbc", [P, S])
        neg_row = sb("neg_row", [1, S], BF16)
        maskt = sb("maskt", [P, S // W])
        key_bias = sb("key_bias", [P, S // W])
        wq = sb("wq", [P, DT, E])
        wk = sb("wk", [P, DT, E])
        wv = sb("wv", [P, DT, E])
        wo = sb("wo", [P, ET, D])
        wb = sb("wb", [P, C // P, C])
        wf = sb("wf", [P, SC, NL])
        bq_sb = sb("bq_sb", [P, ET])
        bk_sb = sb("bk_sb", [P, ET])
        bv_sb = sb("bv_sb", [P, E])
        bo_sb = sb("bo_sb", [P, DT])
        base_sb = sb("base_sb", [P, NL])
        id_sb = sb("id_sb", [P, P])
        sti = sb("sti", [P, NL])
        eye_sb = sb("eye_sb", [P, N * N])
        eye_g = sb("eye_g", [P, N * N])
        gate_sb = sb("gate_sb", [P, 3])
        gt = sb("gt", [P, 8])
        ones = sb("ones", [P, P])
        ones_bf = sb("ones_bf", [1, P], BF16)
        spare = sb("spare", [P, 4 + NC])
        csum = sb("csum", [P, NL])
        bn_a = sb("bn_a", [P, DT, 4, 6])
        mv_a = sb("mv_a", [P, DT, 2])
        ra = sb("ra", [P, 5, DT])
        negm = sb("negm", [P, 2, HPT])
        lnden = sb("lnden", [P, 2, P])
        rden = sb("rden", [P, 2, P])
        bn_b = sb("bn_b", [P, DT, 4, 6])
        mv_b = sb("mv_b", [P, DT, 2])
        rb = sb("rb", [P, 8, DT])
        xt_sb = sb("xt_sb", [P, 2, DT * P])
        wo_tmp = xt_sb
        logit = sb("logit", [P, DT, NL])
        soft = sb("soft", [P, DT, 2, N])
        smx = sb("smx", [P, DT * N])
        sln = sb("sln", [P, DT * N])
        zl = sb("zl", [P, DT, N, N])
        ke = sb("ke", [P, DT, N, N])
        kp = sb("kp", [P, DT, N, N])
        sa = sb("sa", [P, DT, N])
        sv = sb("sv", [P, DT, N])
        ssum = sb("ssum", [P, DT * N])
        cmat = sb("cmat", [P, DT, N, N])
        ccon = sb("ccon", [P, DT, N])
        pre = sb("pre", [P, DT, N])
        post = sb("post", [P, DT, N])
        xpre = sb("xpre", [P, C])
        xpt = sb("xpt", [P, C])
        lgs = xpt
        otile = sb("otile", [P, N, C])

        pr = [ps("pr0"), ps("pr1")]
        s_ps = ps("s_ps")
        st_ps = [ps("st0"), ps("st1")]
        av_ps = ps("av_ps")
        f0 = ps("f0")
        f1 = ps("f1")

        w_loaded = sem("w_loaded")
        x_loaded = [sem(f"x_loaded{t}") for t in range(DT)]
        ctx_loaded = [sem(f"ctx_loaded{i}") for i in range(2)]
        bd_loaded = [sem(f"bd_loaded{i}") for i in range(2)]
        maskbc_loaded = sem("maskbc_loaded")
        maskt_loaded = sem("maskt_loaded")
        zeroed = sem("zeroed")
        consts_ready = sem("consts_ready")
        csum_full = sem("csum_full")
        gates_act = sem("gates_act")
        setup_done = sem("setup_done")
        var_ready = sem("var_ready")
        rs_act = sem("rs_act")
        xstat_ready = sem("xstat_ready")
        xn_ready = sem("xn_ready")
        proj_full = sem("proj_full")
        qk_ready = sem("qk_ready")
        v_ready = sem("v_ready")
        wo_read = sem("wo_read")
        s_full = sem("s_full")
        max_done = sem("max_done")
        st_full = sem("st_full")
        exp_done = sem("exp_done")
        av_full = sem("av_full")
        ln_done = sem("ln_done")
        rden_done = sem("rden_done")
        o_done = sem("o_done")
        gelu_done = sem("gelu_done")
        x1_added = sem("x1_added")
        mask_ready = sem("mask_ready")
        t_full = sem("t_full")
        t_copied = sem("t_copied")
        lg_full = sem("lg_full")
        lg_copied = sem("lg_copied")
        sel_full = sem("sel_full")
        small_req = sem("small_req")
        small_done = sem("small_done")
        xp_first = sem("xp_first")
        xpre_ready = sem("xpre_ready")
        xt_full = sem("xt_full")
        xt_copied = sem("xt_copied")
        y_full = sem("y_full")
        coef_ready = sem("coef_ready")
        acc_ready = sem("acc_ready")
        out_ready = sem("out_ready")
        out_stored = sem("out_stored")
        dve_setup = sem("dve_setup")
        dve_att = sem("dve_att")
        dve_ffn = sem("dve_ffn")

        xr = x.rearrange("b (t p) s -> b t p s", p=P)
        cr = ctx4.rearrange("b (t p) s -> b p t s", p=P)
        outr = out.rearrange("b (t p) s -> b t p s", p=P)

        WEIGHTS = [
            (wq[:], wq_t.rearrange("(t p) e -> p t e", p=P)), (wk[:], wk_t.rearrange("(t p) e -> p t e", p=P)),
            (wv[:], wv_t.rearrange("(t p) e -> p t e", p=P)), (wo[:], wo_t.rearrange("(t p) e -> p t e", p=P)),
            (wb[:], w_branch.rearrange("(t p) e -> p t e", p=P)), (wf[:], wf_t.rearrange("(t p) e -> p t e", p=P)),
            (bq_sb[:], bq), (bk_sb[:], bk), (bv_sb[:], bv), (bo_sb[:], bo), (base_sb[:], base),
            (id_sb[:], ident), (sti[:], stack_i), (eye_sb[:], eye4), (gate_sb[:], gates),
        ]

        T_STEP = 2
        LG_STEP = SC // T_STEP
        SOFT_STEP = LG_STEP + 2
        SINK_STEP = SOFT_STEP + 1
        SINK_PER_STEP = 5
        OUT_STEP = 24
        STEPS = UNITS + 2

        block = ctx.enter_context(nc.Block())

        @block.sync
        def _(sp):
            for dst, src in WEIGHTS:
                sp.dma_start(dst, src).then_inc(w_loaded, 16)

            def load_x(b, t):
                sp.dma_start(xa[:, t, :], xr[bass.ds(b, 1), t].rearrange("o p s -> (o p) s")).then_inc(x_loaded[t], 16)

            def load_ctx(b, c):
                sp.dma_start(ctx_sb[:, c % 2], cr[bass.ds(b, 1), :, :, c * CH:(c + 1) * CH]
                             .rearrange("o p t s -> (o p) t s")).then_inc(ctx_loaded[c % 2], 16)

            def load_masks(b):
                sp.dma_start(maskbc[:], mask_bc[bass.ds(b, 1), :].broadcast_to([P, S])).then_inc(maskbc_loaded, 16)
                sp.dma_start(maskt[:], mask_t[bass.ds(b, 1)].rearrange("o p w -> (o p) w")).then_inc(maskt_loaded, 16)

            def body(b, more):
                for c in range(NC):
                    sp.wait_ge(qk_ready, b * (2 * NC) + 2 * c + 2)
                    for src, dst in ((q_sb, q_bd), (k_sb, k_bd)):
                        for h in range(HPT):
                            rows = slice(h * DH, (h + 1) * DH)
                            sp.dma_start(dst[rows, c % 2].rearrange("p t w h i -> p (t w) h i")[:, :, h, :],
                                         src[rows, c % 2].rearrange("p t (w i) -> p (t w) i", w=WPC)
                                         ).then_inc(bd_loaded[c % 2], 16)
                    if c + 2 < NC:
                        sp.wait_ge(proj_full, b * USES + 3 * c + 3)
                        load_ctx(b, c + 2)
                if more:
                    sp.wait_ge(proj_full, b * USES + PROJ)
                    load_ctx(b + 1, 0)
                    load_ctx(b + 1, 1)
                    for t in range(DT):
                        sp.wait_ge(x1_added, b * (DT * NW) + NW * (t + 1))
                        load_x(b + 1, t)
                    sp.wait_ge(wo_read, (b + 1) * (DT * NW))
                    load_masks(b + 1)

            for t in range(DT):
                load_x(0, t)
            load_ctx(0, 0)
            load_ctx(0, 1)
            load_masks(0)
            with sp.Fori(0, B - 1) as b:
                body(b, True)
            body(B - 1, False)

        @block.gpsimd
        def _(pool):
            pool.memset(q_bd[:], 0.0).then_inc(zeroed, 1)
            pool.memset(k_bd[:], 0.0).then_inc(zeroed, 1)
            pool.memset(spare[:, 2:3], 0.0).then_inc(zeroed, 1)
            pool.wait_ge(zeroed, 3)

            def normalize(b, c):
                if c == 0:
                    pool.wait_ge(xstat_ready, b + 1)
                if c >= 2:
                    pool.wait_ge(proj_full, b * USES + 3 * (c - 2) + 2)
                nc.gpsimd.tensor_tensor(spare[:, 4 + c:5 + c], spare[:, 2:3], spare[:, 2:3], ALU.add)
                for t in range(DT):
                    ins = nc.gpsimd.tensor_scalar(xn[:, c % 2, t, :], xa[:, t, c * CH:(c + 1) * CH],
                                                  ra[:, 2, t:t + 1], ra[:, 4, t:t + 1], ALU.mult, ALU.add)
                ins.then_inc(xn_ready, 1)

            def add_attention(b, t, w):
                n = t * NW + w
                pool.wait_ge(wo_read, b * (DT * NW) + n + 1)
                nc.gpsimd.tensor_tensor(xb[:, t, w * WO_COLS:(w + 1) * WO_COLS],
                                        xa[:, t, w * WO_COLS:(w + 1) * WO_COLS],
                                        wo_tmp[:, n % 2, :], ALU.add).then_inc(x1_added, 1)

            def store(bf, t):
                pool.wait_ge(out_ready, bf * DT + t + 1)
                pool.dma_start(outr[bass.ds(bf, 1), t].rearrange("o p s -> (o p) s"),
                               otile[:].rearrange("p n c -> p (n c)")).then_inc(out_stored, 16)

            def body(b, att, ffn):
                if att:
                    for c in range(NC):
                        normalize(b, c)
                if ffn:
                    for t in range(DT):
                        store(b - 1, t)
                if att:
                    for t in range(DT):
                        for w in range(NW):
                            add_attention(b, t, w)

            body(0, True, False)
            with pool.Fori(1, B) as b:
                body(b, True, True)
            body(B, False, True)
            pool.wait_ge(out_stored, 16 * DT * B)

        @block.tensor
        def _(pe):
            def pr_free(b, n):
                if n < 2:
                    pe.wait_ge(wo_read, b * (DT * NW))
                elif n < 3 * NC + 2:
                    c, kind = divmod(n - 2, 3)
                    if kind < 2:
                        pe.wait_ge(qk_ready, b * (2 * NC) + 2 * c + kind + 1)
                    else:
                        pe.wait_ge(v_ready, b * NC + c + 1)
                else:
                    pe.wait_ge(wo_read, b * (DT * NW) + n - 2 - 3 * NC + 1)

            def project(b, c, kind, first):
                n = 3 * c + kind
                if not (first and n < 2):
                    pr_free(b, n)
                bank = pr[n % 2]
                if kind < 2:
                    pe.wait_ge(xn_ready, b * NC + c + 1)
                    w = (wq, wk)[kind]
                    for et in range(ET):
                        for t in range(DT):
                            ins = nc.tensor.matmul(bank[:, et * CH:(et + 1) * CH], w[:, t, et * P:(et + 1) * P],
                                                   xn[:, c % 2, t, :], start=(t == 0), stop=(t == DT - 1))
                else:
                    pe.wait_ge(ctx_loaded[c % 2], b * (8 * NC) + 16 * (c // 2 + 1))
                    for w in range(WPC):
                        for t in range(DT):
                            ins = nc.tensor.matmul(bank[:, w * E:(w + 1) * E],
                                                   ctx_sb[:, c % 2, t, w * W:(w + 1) * W], wv[:, t, :],
                                                   start=(t == 0), stop=(t == DT - 1))
                ins.then_inc(proj_full, 1)

            def place(u):
                c, r = divmod(u, UPC)
                return c, r // ET, r % ET

            def scores(b, u, first):
                c, w, et = place(u)
                if u % UPC == 0:
                    pe.wait_ge(bd_loaded[c % 2], b * (BD * NC // 2) + BD * (c // 2 + 1))
                if u == 0:
                    pe.wait_ge(mask_ready, b + 1)
                if not (first and u == 0):
                    pe.wait_ge(max_done, b * UNITS + u)
                win = slice(w * W, (w + 1) * W)
                nc.tensor.matmul(s_ps[:], q_sb[:, c % 2, et, win],
                                 k_bd[:, c % 2, et, w].rearrange("p h j -> p (h j)"), start=True, stop=False)
                g = c * WPC + w
                nc.tensor.matmul(s_ps[:].rearrange("p (h j) -> p h j", h=HPT), ones_bf[:],
                                 bcast(neg_row[:, g * W:(g + 1) * W], 1, HPT), start=False, stop=True
                                 ).then_inc(s_full, 1)

            def scores_t(b, u, first):
                c, w, et = place(u)
                if not (first and u < 2):
                    pe.wait_ge(exp_done, b * UNITS + u - 1)
                win = slice(w * W, (w + 1) * W)
                bank = st_ps[u % 2]
                nc.tensor.matmul(bank[:], k_sb[:, c % 2, et, win],
                                 q_bd[:, c % 2, et, w].rearrange("p h i -> p (h i)"), start=True, stop=False)
                pe.wait_ge(max_done, b * UNITS + u + 1)
                for h in range(HPT):
                    ins = nc.tensor.matmul(bank[:, h * W:(h + 1) * W],
                                           negm[:, u % 2, h:h + 1].broadcast_to([P, P]), id_sb[:],
                                           start=False, stop=(h == HPT - 1))
                ins.then_inc(st_full, 1)

            def values(b, u, first):
                c, w, et = place(u)
                pe.wait_ge(exp_done, b * UNITS + u + 1)
                if u % UPC == 0:
                    pe.wait_ge(v_ready, b * NC + c + 1)
                if not (first and u == 0):
                    pe.wait_ge(o_done, b * UNITS + u)
                for h in range(HPT):
                    rows = slice(h * DH, (h + 1) * DH)
                    nc.tensor.matmul(av_ps[rows, 0:W], v_t[:, c % 2, w, et * P + h * DH:et * P + (h + 1) * DH],
                                     probs[:, u % 2, h * W:(h + 1) * W], start=True, stop=True)
                for h in range(HPT):
                    rows = slice(h * DH, (h + 1) * DH)
                    ins = nc.tensor.matmul(av_ps[rows, W:2 * W], ones[:, 0:DH],
                                           probs[:, u % 2, h * W:(h + 1) * W], start=True, stop=True)
                ins.then_inc(av_full, 1)

            def output(b, t, w):
                n = PROJ + t * NW + w
                pr_free(b, n)
                if t == 0:
                    pe.wait_ge(gelu_done, b * (ET * NW) + ET * (w + 1))
                for et in range(ET):
                    ins = nc.tensor.matmul(pr[n % 2][:], wo[:, et, t * P:(t + 1) * P],
                                           o_sb[:, et, w * WO_COLS:(w + 1) * WO_COLS],
                                           start=(et == 0), stop=(et == ET - 1))
                ins.then_inc(proj_full, 1)

            def transpose_x(bf, k):
                if k == 0:
                    pe.wait_ge(x1_added, (bf + 1) * (DT * NW))
                else:
                    pe.wait_ge(t_copied, bf * SC + k)
                for t in range(DT):
                    ins = nc.tensor.transpose(f0[:, t * P:(t + 1) * P], xb[:, t, k * P:(k + 1) * P], id_sb[:])
                ins.then_inc(t_full, 1)

            def logits(bf, k):
                pe.wait_ge(t_copied, bf * SC + k + 1)
                g = k % 4
                nc.tensor.matmul(f1[g * NL:(g + 1) * NL, :], wf[:, k, :], xt_sb[:, k % 2, :],
                                 start=(k < 4), stop=(k >= SC - 4)).then_inc(lg_full, 1)

            def select(bf):
                pe.wait_ge(lg_copied, bf + 1)
                pe.wait_ge(t_copied, (bf + 1) * SC)
                for t in range(DT):
                    ins = nc.tensor.matmul(f0[:, t * NL:(t + 1) * NL], lgs[:, t * P:(t + 1) * P], sti[:],
                                           start=True, stop=True)
                ins.then_inc(sel_full, 1)

            def transpose_pre(bf, t):
                pe.wait_ge(xpre_ready, bf * DT + t + 1)
                if t:
                    pe.wait_ge(xt_copied, bf * DT + t)
                for j in range(C // P):
                    ins = nc.tensor.transpose(f0[:, j * P:(j + 1) * P], xpre[:, j * P:(j + 1) * P], id_sb[:])
                ins.then_inc(xt_full, 1)

            def branch(bf, t):
                pe.wait_ge(xt_copied, bf * DT + t + 1)
                if t:
                    pe.wait_ge(out_ready, bf * DT + t)
                for j in range(C // P):
                    ins = nc.tensor.matmul(f1[:], xpt[:, j * P:(j + 1) * P], wb[:, j, :],
                                           start=(j == 0), stop=(j == C // P - 1))
                ins.then_inc(y_full, 1)

            def body(b, att, ffn, first=False):
                bf = b - 1
                if att:
                    for kind in range(3):
                        project(b, 0, kind, first)
                for k in range(STEPS):
                    if att:
                        if k < UNITS:
                            scores(b, k, first)
                        if 1 <= k <= UNITS:
                            scores_t(b, k - 1, first)
                        if k >= 2:
                            values(b, k - 2, first)
                        c, r = divmod(k, UPC)
                        if c + 1 < NC and r < 3:
                            project(b, c + 1, r, first)
                    if ffn:
                        for j in range(T_STEP * k, min(T_STEP * k + T_STEP, SC)):
                            transpose_x(bf, j)
                            if j:
                                logits(bf, j - 1)
                        if k == LG_STEP:
                            logits(bf, SC - 1)
                        if k == LG_STEP + 1:
                            select(bf)
                        t, r = divmod(k - OUT_STEP, 2)
                        if 0 <= t < DT:
                            if r == 0:
                                transpose_pre(bf, t)
                            else:
                                branch(bf, t)
                if att:
                    for t in range(DT):
                        for w in range(NW):
                            output(b, t, w)

            pe.wait_ge(w_loaded, 16 * len(WEIGHTS))
            pe.wait_ge(consts_ready, 2)
            for k in range(SC):
                ins = nc.tensor.matmul(f0[:, 0:NL], ones[:], wf[:, k, :], start=(k == 0), stop=(k == SC - 1))
            ins.then_inc(csum_full, 1)
            pe.wait_ge(setup_done, 1)
            pe.wait_ge(zeroed, 3)
            body(0, True, False, first=True)
            with pe.Fori(1, B) as b:
                body(b, True, True)
            body(B, False, True)

        @block.scalar
        def _(act):
            exp_k = (ke[:], zl[:], ACT.Exp, 1.0)
            ln_sum = (sln[:], ssum[:], ACT.Ln, 1.0)
            small_list = [(rb[:, 1, :], rb[:, 0, :], ACT.Ln, 1.0), (rb[:, 2, :], rb[:, 1, :], ACT.Exp, -0.5),
                          (rb[:, 1, :], rb[:, 4, :], ACT.Ln, 1.0), (rb[:, 2, :], rb[:, 1, :], ACT.Exp, -0.5),
                          (soft[:], soft[:], ACT.Exp, 1.0),
                          exp_k, ln_sum, exp_k, ln_sum, exp_k]
            a_t, v_t4 = (v[:].rearrange("p t i -> p (t i)") for v in (sa, sv))
            for _ in RETURNS:
                small_list += [(sln[:], v_t4, ACT.Ln, 1.0), (sln[:], a_t, ACT.Ln, 1.0), exp_k]
            small_at = {DT: 4, SOFT_STEP: 6}
            for it in RETURNS:
                k = SINK_STEP + (it - 1) // SINK_PER_STEP
                small_at[k] = small_at.get(k, 0) + 3

            def xstat(b):
                act.wait_ge(var_ready, b + 1)
                nc.scalar.activation(ra[:, 1, :], ra[:, 0, :], ACT.Ln).then_inc(rs_act, 1)
                act.wait_ge(rs_act, 2 * b + 1)
                nc.scalar.activation(ra[:, 3, :], ra[:, 1, :], ACT.Exp, scale=-0.5).then_inc(rs_act, 1)

            def read_qk(b, c, kind, first):
                n = 3 * c + kind
                act.wait_ge(proj_full, b * USES + n + 1)
                if not (first and c < 2):
                    act.wait_ge(st_full, b * UNITS + UPC * (c - 1))
                    if kind == 0:
                        act.wait_ge(s_full, b * UNITS + UPC * (c - 1))
                dst, bias = ((q_sb, bq_sb), (k_sb, bk_sb))[kind]
                for et in range(ET):
                    ins = nc.scalar.activation(dst[:, c % 2, et, :], pr[n % 2][:, et * CH:(et + 1) * CH],
                                               ACT.Identity, bias=bias[:, et:et + 1])
                ins.then_inc(qk_ready, 1)

            def exp_scores(b, u, first):
                g = u // ET
                act.wait_ge(st_full, b * UNITS + u + 1)
                if not (first and u < 2):
                    act.wait_ge(av_full, b * UNITS + u - 1)
                nc.scalar.activation(probs[:, u % 2, :], st_ps[u % 2][:], ACT.Exp,
                                     bias=key_bias[:, g:g + 1], scale=SCALE).then_inc(exp_done, 1)

            def inverse_den(b, u, first):
                act.wait_ge(av_full, b * UNITS + u + 1)
                if not (first and u < 2):
                    act.wait_ge(o_done, b * UNITS + u - 1)
                nc.scalar.activation(lnden[:, u % 2, :], av_ps[:, W:2 * W], ACT.Ln).then_inc(ln_done, 1)
                act.wait_ge(ln_done, b * UNITS + u + 1)
                nc.scalar.activation(rden[:, u % 2, :], lnden[:, u % 2, :], ACT.Exp, scale=-1.0
                                     ).then_inc(rden_done, 1)

            def gelu(b):
                act.wait_ge(o_done, (b + 1) * UNITS)
                for w in range(NW):
                    for et in range(ET):
                        part = o_sb[:, et, w * WO_COLS:(w + 1) * WO_COLS]
                        nc.scalar.activation(part, part, ACT.Gelu).then_inc(gelu_done, 1)

            def copy_t(bf, k):
                act.wait_ge(t_full, bf * SC + k + 1)
                if k >= 2:
                    act.wait_ge(lg_full, bf * SC + k - 1)
                nc.scalar.activation(xt_sb[:, k % 2, :], f0[:], ACT.Copy).then_inc(t_copied, 1)

            def copy_lg(bf):
                act.wait_ge(lg_full, (bf + 1) * SC)
                nc.scalar.activation(lgs[:], f1[:], ACT.Copy).then_inc(lg_copied, 1)

            small = [0]

            def small_step(bf, dst, src, func, scale=1.0):
                small[0] += 1
                act.wait_ge(small_req, bf * SMALL + small[0])
                nc.scalar.activation(dst, src, func, scale=scale).then_inc(small_done, 1)

            def first_products(bf, t):
                if t == 0:
                    act.wait_ge(coef_ready, 2 * bf + 1)
                else:
                    act.wait_ge(xt_full, bf * DT + t)
                nc.scalar.activation(xpre[:], xb[:, t, 0:C], ACT.Identity, bias=rb[:, 6, t:t + 1],
                                     scale=pre[:, t, 0:1]).then_inc(xp_first, 1)

            def copy_pre(bf, t):
                act.wait_ge(xt_full, bf * DT + t + 1)
                if t:
                    act.wait_ge(y_full, bf * DT + t)
                nc.scalar.activation(xpt[:], f0[:], ACT.Copy).then_inc(xt_copied, 1)

            def first_out(bf, t):
                if t == 0:
                    act.wait_ge(coef_ready, 2 * bf + 2)
                else:
                    act.wait_ge(out_stored, 16 * (bf * DT + t))
                for i in range(N):
                    nc.scalar.activation(otile[:, i, :], xb[:, t, 0:C], ACT.Identity, bias=ccon[:, t, i:i + 1],
                                         scale=cmat[:, t, i, 0:1]).then_inc(acc_ready, 1)

            def small_steps(bf, n):
                for _ in range(n):
                    small_step(bf, *small_list[small[0]])

            def body(b, att, ffn, first=False):
                bf = b - 1
                small[0] = 0
                if att:
                    xstat(b)
                    for kind in range(2):
                        read_qk(b, 0, kind, first)
                for k in range(STEPS):
                    if att:
                        if 1 <= k <= UNITS:
                            exp_scores(b, k - 1, first)
                        if k >= 2:
                            inverse_den(b, k - 2, first)
                        c, r = divmod(k, UPC)
                        if c + 1 < NC and r < 2:
                            read_qk(b, c + 1, r, first)
                    if ffn:
                        for j in range(T_STEP * k, min(T_STEP * k + T_STEP, SC)):
                            copy_t(bf, j)
                        if k == LG_STEP:
                            copy_lg(bf)
                        if k in small_at:
                            small_steps(bf, small_at[k])
                        t, r = divmod(k - OUT_STEP, 2)
                        if r == 1 and 0 <= t + 1 < DT and t >= -1:
                            first_products(bf, t + 1)
                        if 0 <= t < DT:
                            if r == 0:
                                copy_pre(bf, t)
                            else:
                                first_out(bf, t)
                if ffn:
                    assert small[0] == SMALL
                if att:
                    gelu(b)
                if ffn:
                    act.wait_ge(out_stored, (bf + 1) * (16 * DT))

            act.wait_ge(w_loaded, 16 * len(WEIGHTS))
            nc.scalar.activation(gt[:, 0:2], gate_sb[:, 0:2], ACT.Tanh).then_inc(gates_act, 1)
            nc.scalar.activation(gt[:, 4:5], gate_sb[:, 2:3], ACT.Exp, scale=-1.0).then_inc(gates_act, 1)
            act.wait_ge(setup_done, 1)
            body(0, True, False, first=True)
            with act.Fori(1, B) as b:
                body(b, True, True)
            body(B, False, True)

        @block.vector
        def _(dve):
            setup = Chain(dve, dve_setup, 7)
            ca = Chain(dve, dve_att, DVE_ATT)
            cf = Chain(dve, dve_ffn, DVE_FFN)

            def newton(chain, r, guess, value, work):
                chain.link(nc.vector.tensor_tensor(work, guess, guess, ALU.mult))
                chain.link(nc.vector.tensor_tensor(work, work, value, ALU.mult))
                chain.link(nc.vector.tensor_scalar(work, work, -0.5, 1.5, ALU.mult, ALU.add))
                chain.link(nc.vector.tensor_tensor(r, guess, work, ALU.mult))

            def xstat(b):
                for t in range(DT):
                    dve.wait_ge(x_loaded[t], 16 * b + 16)
                    for j in range(4):
                        ins = nc.vector.bn_stats(bn_a[:, t, j, :], xa[:, t, j * 512:(j + 1) * 512])
                ca.link(ins)
                nc.vector.memset(spare[:, 0:1], 0.0)
                for t in range(DT):
                    ins = nc.vector.bn_aggr(mv_a[:, t, :], bn_a[:, t].rearrange("p j s -> p (j s)"))
                ca.link(ins)
                nc.vector.tensor_scalar(ra[:, 0, :], mv_a[:, :, 1], LN_EPS, None, ALU.add).then_inc(var_ready, 1)
                dve.wait_ge(maskbc_loaded, 16 * b + 16)
                dve.wait_ge(maskt_loaded, 16 * b + 16)
                nc.vector.tensor_scalar(neg_row[:], maskbc[0:1, :], 0.0, NEG, ALU.is_le, ALU.mult)
                nc.vector.tensor_scalar(key_bias[:], maskt[:], 0.0, NEG * SCALE, ALU.is_le, ALU.mult
                                        ).then_inc(mask_ready, 1)
                dve.wait_ge(rs_act, 2 * b + 2)
                newton(ca, ra[:, 2, :], ra[:, 3, :], ra[:, 0, :], ra[:, 1, :])
                nc.vector.scalar_tensor_tensor(out=ra[:, 4, :], in0=mv_a[:, :, 0], scalar=-1.0, in1=ra[:, 2, :],
                                               op0=ALU.mult, op1=ALU.mult).then_inc(xstat_ready, 1)

            def read_v(b, c, first):
                n = 3 * c + 2
                dve.wait_ge(proj_full, b * USES + n + 1)
                if not (first and c < 2):
                    dve.wait_ge(av_full, b * UNITS + UPC * (c - 1))
                nc.vector.tensor_tensor(v_t[:, c % 2], pr[n % 2][:].rearrange("p (w e) -> p w e", w=WPC),
                                        bcast(bv_sb[:], 1, WPC), ALU.add).then_inc(v_ready, 1)

            def maximum(b, u, first):
                dve.wait_ge(s_full, b * UNITS + u + 1)
                if not (first and u < 2):
                    dve.wait_ge(st_full, b * UNITS + u - 1)
                nc.vector.tensor_reduce(negm[:, u % 2, :], s_ps[:].rearrange("p (h j) -> p h j", h=HPT),
                                        AX.X, ALU.max, negate=True).then_inc(max_done, 1)

            def divide(b, u):
                g, et = divmod(u, ET)
                dve.wait_ge(rden_done, b * UNITS + u + 1)
                if u == 0:
                    dve.wait_ge(proj_full, b * USES)
                nc.vector.tensor_tensor(o_sb[:, et, g * W:(g + 1) * W], av_ps[:, 0:W], rden[:, u % 2, :], ALU.mult
                                        ).then_inc(o_done, 1)

            def read_wo(b, t, w, first):
                n = t * NW + w
                dve.wait_ge(proj_full, b * USES + PROJ + n + 1)
                if not (first and n < 2):
                    dve.wait_ge(x1_added, b * (DT * NW) + n - 1)
                nc.vector.scalar_tensor_tensor(out=wo_tmp[:, n % 2, :], in0=pr[(PROJ + n) % 2][:],
                                               scalar=bo_sb[:, t:t + 1], in1=maskbc[:, w * WO_COLS:(w + 1) * WO_COLS],
                                               op0=ALU.add, op1=ALU.mult).then_inc(wo_read, 1)

            small = [0]

            def ask(bf, ins):
                small[0] += 1
                ins.then_inc(small_req, 1)
                dve.wait_ge(small_done, bf * SMALL + small[0])

            def stat_b(bf, t):
                if t == 0:
                    dve.wait_ge(x1_added, (bf + 1) * (DT * NW))
                for j in range(4):
                    ins = nc.vector.bn_stats(bn_b[:, t, j, :], xb[:, t, j * 512:(j + 1) * 512])
                cf.link(ins)
                nc.vector.memset(spare[:, 0:1], 0.0)
                cf.link(nc.vector.bn_aggr(mv_b[:, t, :], bn_b[:, t].rearrange("p j s -> p (j s)")))

            def stat_finish(bf):
                ask(bf, nc.vector.tensor_scalar(rb[:, 0, :], mv_b[:, :, 1], LN_EPS, None, ALU.add))
                ask(bf, nc.vector.tensor_scalar(rb[:, 7, :], mv_b[:, :, 0], -1.0, None, ALU.mult))
                newton(cf, rb[:, 3, :], rb[:, 2, :], rb[:, 0, :], rb[:, 1, :])
                cf.link(nc.vector.tensor_tensor(rb[:, 4, :], rb[:, 3, :], rb[:, 3, :], ALU.mult))
                cf.link(nc.vector.tensor_tensor(rb[:, 4, :], rb[:, 4, :], mv_b[:, :, 1], ALU.mult))
                ask(bf, nc.vector.tensor_scalar(rb[:, 4, :], rb[:, 4, :], RMS_EPS, None, ALU.add))
                ask(bf, nc.vector.tensor_tensor(rb[:, 6, :], rb[:, 7, :], rb[:, 3, :], ALU.mult))
                newton(cf, rb[:, 5, :], rb[:, 2, :], rb[:, 4, :], rb[:, 1, :])
                cf.link(nc.vector.tensor_tensor(rb[:, 5, :], rb[:, 5, :], rb[:, 3, :], ALU.mult))

            l_t = sln[:].rearrange("p (t i) -> p t i", t=DT)
            kcol = ke[:].rearrange("p t i j -> p t j i")
            zcol = zl[:].rearrange("p t i j -> p t j i")
            s_t = ssum[:].rearrange("p (t i) -> p t i", t=DT)
            m_t = smx[:].rearrange("p (t i) -> p t i", t=DT)

            def over_j(v):
                return bcast(v, 3, N)

            def over_i(v):
                return bcast(v, 2, N)

            def logits_and_softmax(bf):
                dve.wait_ge(sel_full, bf + 1)
                for t in range(DT):
                    ins = nc.vector.scalar_tensor_tensor(out=logit[:, t, :], in0=csum[:], scalar=rb[:, 7, t:t + 1],
                                                         in1=f0[:, t * NL:(t + 1) * NL], op0=ALU.mult, op1=ALU.add)
                cf.link(ins)
                for t in range(DT):
                    ins = nc.vector.scalar_tensor_tensor(out=logit[:, t, :], in0=logit[:, t, :],
                                                         scalar=rb[:, 5, t:t + 1], in1=base_sb[:],
                                                         op0=ALU.mult, op1=ALU.add)
                cf.link(ins)
                lpp = logit[:, :, N * N:N * N + 2 * N].rearrange("p t (k n) -> p t k n", k=2)
                m8 = kp[:].rearrange("p t i j -> p (t i j)")[:, 0:2 * DT].rearrange("p (t k) -> p t k", t=DT)
                cf.link(nc.vector.tensor_reduce(m8, lpp, AX.X, ALU.max))
                ask(bf, nc.vector.tensor_tensor(soft[:], lpp, bcast(m8, 3, N), ALU.subtract))
                cf.link(nc.vector.tensor_reduce(m8, soft[:], AX.X, ALU.add))
                cf.link(nc.vector.reciprocal(m8, m8))
                cf.link(nc.vector.tensor_tensor(soft[:], soft[:], bcast(m8, 3, N), ALU.mult))
                nc.vector.tensor_tensor(pre[:], soft[:, :, 0, :], bcast(rb[:, 3, :], 2, N), ALU.mult
                                        ).then_inc(coef_ready, 1)
                cf.link(nc.vector.tensor_scalar(post[:], soft[:, :, 1, :], gt[:, 1:2], None, ALU.mult))
                cf.link(nc.vector.tensor_scalar(zl[:].rearrange("p t i j -> p t (i j)"), logit[:, :, 0:N * N],
                                                1.0 / TAU, None, ALU.mult))
                for z, e in ((zl[:], ke[:]), (zcol, kcol)):
                    cf.link(nc.vector.tensor_reduce(m_t, z, AX.X, ALU.max))
                    ask(bf, nc.vector.tensor_tensor(z, z, bcast(m_t, 3, N), ALU.subtract))
                    ask(bf, nc.vector.tensor_reduce(s_t, e, AX.X, ALU.add))
                    less = nc.vector.tensor_tensor(z, z, bcast(l_t, 3, N), ALU.subtract)
                    if e is kcol:
                        ask(bf, less)
                    else:
                        cf.link(less)

            def sinkhorn(bf, it):
                kpc = kp[:].rearrange("p t i j -> p t j i")
                if it % SEG == 1:
                    cf.link(nc.vector.tensor_reduce(s_t, ke[:], AX.X, ALU.add))
                else:
                    cf.link(nc.vector.tensor_tensor(kp[:], ke[:], over_i(sv[:]), ALU.mult))
                    cf.link(nc.vector.tensor_reduce(s_t, kp[:], AX.X, ALU.add))
                cf.link(nc.vector.reciprocal(sa[:], s_t))
                cf.link(nc.vector.tensor_tensor(kp[:], ke[:], over_j(sa[:]), ALU.mult))
                cf.link(nc.vector.tensor_reduce(s_t, kpc, AX.X, ALU.add))
                made = nc.vector.reciprocal(sv[:], s_t)
                if it % SEG or it == ITERS - 1:
                    cf.link(made)
                else:
                    ask(bf, made)
                    ask(bf, nc.vector.tensor_tensor(zl[:], zl[:], over_i(l_t), ALU.add))
                    ask(bf, nc.vector.tensor_tensor(zl[:], zl[:], over_j(l_t), ALU.add))

            def coefficients(bf):
                cf.link(nc.vector.tensor_tensor(kp[:], ke[:], over_j(sa[:]), ALU.mult))
                cf.link(nc.vector.tensor_tensor(kp[:], kp[:], over_i(sv[:]), ALU.mult))
                flat = kp[:].rearrange("p t i j -> p t (i j)")
                cf.link(nc.vector.tensor_scalar(flat, flat, gt[:, 2:3], None, ALU.mult))
                cf.link(nc.vector.tensor_tensor(flat, flat, bcast(eye_g[:], 1, DT), ALU.add))
                cf.link(nc.vector.tensor_scalar(flat, flat, gt[:, 1:2], None, ALU.mult))
                cf.link(nc.vector.tensor_reduce(s_t, kp[:], AX.X, ALU.add))
                cf.link(nc.vector.tensor_tensor(ccon[:], s_t, bcast(rb[:, 6, :], 2, N), ALU.mult))
                cf.link(nc.vector.tensor_tensor(flat, flat, bcast(rb[:, 3, :], 2, N * N), ALU.mult))
                nc.vector.tensor_tensor(cmat[:].rearrange("p t i j -> p t (i j)"), flat, bcast(eye_sb[:], 1, DT),
                                        ALU.add).then_inc(coef_ready, 1)
                dve.wait_ge(coef_ready, 2 * bf + 2)

            def make_xpre(bf, t):
                dve.wait_ge(xp_first, bf * DT + t + 1)
                for n in range(1, N):
                    ins = nc.vector.scalar_tensor_tensor(out=xpre[:], in0=xb[:, t, n * C:(n + 1) * C],
                                                         scalar=pre[:, t, n:n + 1], in1=xpre[:],
                                                         op0=ALU.mult, op1=ALU.add)
                    if n < N - 1:
                        cf.link(ins)
                ins.then_inc(xpre_ready, 1)

            def make_out(bf, t):
                for j in range(1, N):
                    for i in range(N):
                        if j == 1:
                            dve.wait_ge(acc_ready, bf * (DT * N) + t * N + i + 1)
                        ins = nc.vector.scalar_tensor_tensor(out=otile[:, i, :], in0=xb[:, t, j * C:(j + 1) * C],
                                                             scalar=cmat[:, t, i, j:j + 1], in1=otile[:, i, :],
                                                             op0=ALU.mult, op1=ALU.add)
                    cf.link(ins)
                dve.wait_ge(y_full, bf * DT + t + 1)
                for i in range(N):
                    ins = nc.vector.scalar_tensor_tensor(out=otile[:, i, :], in0=f1[:], scalar=post[:, t, i:i + 1],
                                                         in1=otile[:, i, :], op0=ALU.mult, op1=ALU.add)
                ins.then_inc(out_ready, 1)

            def body(b, att, ffn, first=False):
                bf = b - 1
                small[0] = 0
                if att:
                    ca.start(b)
                    xstat(b)
                    read_v(b, 0, first)
                if ffn:
                    cf.start(bf)
                for k in range(STEPS):
                    if att:
                        if k < UNITS:
                            maximum(b, k, first)
                        if k >= 2:
                            divide(b, k - 2)
                        c, r = divmod(k, UPC)
                        if c + 1 < NC and r == 2:
                            read_v(b, c + 1, first)
                    if ffn:
                        if k < DT:
                            stat_b(bf, k)
                        if k == DT:
                            stat_finish(bf)
                        if k == SOFT_STEP:
                            logits_and_softmax(bf)
                        if k >= SINK_STEP:
                            i0 = 1 + SINK_PER_STEP * (k - SINK_STEP)
                            for it in range(i0, min(i0 + SINK_PER_STEP, ITERS)):
                                sinkhorn(bf, it)
                            if i0 < ITERS <= i0 + SINK_PER_STEP:
                                coefficients(bf)
                        t, r = divmod(k - OUT_STEP, 2)
                        if r == 1 and 0 <= t + 1 < DT and t >= -1:
                            make_xpre(bf, t + 1)
                        if r == 1 and 0 <= t < DT:
                            make_out(bf, t)
                if ffn:
                    cf.end()
                if att:
                    for t in range(DT):
                        for w in range(NW):
                            read_wo(b, t, w, first)
                    ca.end()

            nc.vector.memset(ones[:], 1.0).then_inc(consts_ready, 1)
            nc.vector.memset(ones_bf[:], 1.0).then_inc(consts_ready, 1)
            dve.wait_ge(w_loaded, 16 * len(WEIGHTS))
            dve.wait_ge(csum_full, 1)
            setup.link(nc.vector.tensor_copy(csum[:], f0[:, 0:NL]))
            dve.wait_ge(gates_act, 2)
            setup.link(nc.vector.tensor_scalar(gt[:, 5:6], gt[:, 4:5], 1.0, None, ALU.add))
            setup.link(nc.vector.reciprocal(gt[:, 2:3], gt[:, 5:6]))
            setup.link(nc.vector.tensor_scalar(gt[:, 3:4], gt[:, 2:3], -1.0, 1.0, ALU.mult, ALU.add))
            setup.link(nc.vector.tensor_scalar(eye_g[:], eye_sb[:], gt[:, 3:4], None, ALU.mult))
            setup.link(nc.vector.tensor_scalar(wo[:].rearrange("p t e -> p (t e)"),
                                               wo[:].rearrange("p t e -> p (t e)"), gt[:, 0:1], None, ALU.mult))
            setup.link(nc.vector.tensor_scalar(bo_sb[:], bo_sb[:], gt[:, 0:1], None, ALU.mult))
            setup.end()
            nc.vector.memset(spare[:, 0:1], 0.0).then_inc(setup_done, 1)
            body(0, True, False, first=True)
            with dve.Fori(1, B) as b:
                body(b, True, True)
            body(B, False, True)


_OUTS = [((B, D, S), "float32")]


def kernel(x, ctx_4096, mask_Bx1x4096_ff1, g_xattn, g_ffn, L0_xattn_Wq, L0_xattn_bq, L0_xattn_Wk, L0_xattn_bk,
           L0_xattn_Wv, L0_xattn_bv, L0_xattn_Wo, L0_xattn_bo, L0_ffn_W_res, L0_ffn_W_pre, L0_ffn_W_post,
           L0_ffn_H_res_base, L0_ffn_H_pre_base, L0_ffn_H_post_base, L0_ffn_gate, L0_ffn_W_branch):
    import numpy as np
    import concourse.bacc as _bacc
    from concourse import mybir as _mybir
    from concourse.bass_utils import run_bass_kernel_spmd as _run

    A = np.asarray

    def rows(v):
        return np.broadcast_to(A(v).reshape(1, -1), (P, A(v).size))

    mask = A(mask_Bx1x4096_ff1)[:, 0, :]
    pad = np.zeros((NL - N * N - 2 * N, S), np.float32)
    ordered = [
        A(x), A(ctx_4096), mask, mask.reshape(B, S // W, W).transpose(0, 2, 1),
        np.concatenate([rows(g_xattn), rows(g_ffn), rows(L0_ffn_gate)], axis=1),
        A(L0_xattn_Wq).T, A(L0_xattn_bq).reshape(ET, P).T, A(L0_xattn_Wk).T, A(L0_xattn_bk).reshape(ET, P).T,
        A(L0_xattn_Wv).T, rows(L0_xattn_bv), A(L0_xattn_Wo).T, A(L0_xattn_bo).reshape(DT, P).T,
        np.concatenate([A(L0_ffn_W_res), A(L0_ffn_W_pre), A(L0_ffn_W_post), pad], axis=0).T,
        np.concatenate([rows(L0_ffn_H_res_base), rows(L0_ffn_H_pre_base), rows(L0_ffn_H_post_base),
                        np.zeros((P, NL - N * N - 2 * N), np.float32)], axis=1),
        A(L0_ffn_W_branch), np.eye(P, dtype=np.float32), np.tile(np.eye(NL, dtype=np.float32), (4, 1)),
        rows(np.eye(N, dtype=np.float32)),
    ]
    nc = _bacc.Bacc("TRN2", target_bir_lowering=False, num_devices=1)
    arrays, args = {}, []
    for i, a in enumerate(ordered):
        a = np.ascontiguousarray(a)
        arrays[f"in_{i}_dram"] = a
        args.append(nc.dram_tensor(f"in_{i}_dram", a.shape, _mybir.dt.from_np(a.dtype), kind="ExternalInput").ap())
    for i, (shape, dtype) in enumerate(_OUTS):
        dt = _mybir.dt.from_np(np.dtype(dtype))
        args.append(nc.dram_tensor(f"out_{i}_dram", shape, dt, kind="ExternalOutput").ap())
    program(nc, *args)
    r = _run(nc, [arrays], core_ids=[0])
    return tuple(r.results[0][f"out_{i}_dram"] for i in range(len(_OUTS)))[0]
```

```python
from contextlib import ExitStack

import concourse.bass as bass
from concourse import mybir

F32 = mybir.dt.float32
BF16 = mybir.dt.bfloat16
ALU = mybir.AluOpType
ACT = mybir.ActivationFunctionType
AX = mybir.AxisListType

P = 128
B, D, S = 8, 512, 2048
W = 128
HEADS, DH = 8, 32
E = HEADS * DH
DT = D // P
ET = E // P
HPT = P // DH
CH = 4 * W
NC = S // CH
WPC = CH // W
UNITS = S // W * ET
UPC = UNITS // NC
WO_COLS = 512
NW = S // WO_COLS
SCALE = float(DH) ** -0.5
NEG = -float(2 ** 40)
LN_EPS = 1e-5
RMS_EPS = 1.1920929e-07
N = 4
C = S // N
NL = 32
ITERS = 50
TAU = 0.1
SEG = 10

FIRST_USES = [("v", 0, 0), ("v", 0, 1), ("q", 0, 0), ("q", 0, 1), ("k", 0, 0), ("k", 0, 1)]
PROJ_USES = FIRST_USES + [(kind, c, i) for c in range(1, NC) for kind in "qkv" for i in range(2)]
PROJ = len(PROJ_USES)
USES = PROJ + DT * NW
ROWS = 3 * DH
STACK_DMAS = 6 * HPT + 1
STACKED = 16 * STACK_DMAS
SC = S // P
RETURNS = range(SEG, ITERS, SEG)
SMALL = 10 + 3 * len(RETURNS)
DVE_ATT = 6
DVE_FFN = 355


def use(kind, c, i):
    return PROJ_USES.index((kind, c, i))


def bcast(ap, axis, n):
    ap = ap.unsqueeze(axis)
    shape = list(ap.shape)
    shape[axis] = n
    return ap.broadcast_to(shape)


class Chain:

    def __init__(self, eng, sem, per_batch):
        self.eng, self.sem, self.per, self.n, self.base = eng, sem, per_batch, 0, 0

    def start(self, b):
        self.n, self.base = 0, b * self.per

    def link(self, ins):
        self.n += 1
        ins.then_inc(self.sem, 1)
        self.eng.wait_ge(self.sem, self.base + self.n)

    def end(self):
        assert self.n == self.per, (self.n, self.per)


def program(nc, x, ctx4, mask_bc, mask_t, gates, wq_t, bq, wk_t, bk, wv_t, bv, wo_t, bo, wf_t, base,
            w_branch, ident, stack_i, eye4, out):
    with ExitStack() as ctx:
        def sb(name, shape, dt=F32):
            return ctx.enter_context(nc.sbuf_tensor(name, shape, dt))

        def ps(name):
            return ctx.enter_context(nc.psum_tensor(name, [P, 512], F32))

        def sem(name):
            return ctx.enter_context(nc.semaphore(name))

        xa = sb("xa", [P, DT, S])
        xb = sb("xb", [P, DT, S])
        ctx_raw = sb("ctx_raw", [P, DT, CH])
        ctx_hl = sb("ctx_hl", [P, 2, DT, CH], BF16)
        x_hl = sb("x_hl", [P, 2, DT, CH], BF16)
        xn = sb("xn", [P, 2, CH])
        q_hl = sb("q_hl", [P, 2, ET, CH], BF16)
        k_hl = sb("k_hl", [P, 2, ET, CH], BF16)
        q_st = sb("q_st", [P, 2, ET, HPT, CH], BF16)
        k_st = sb("k_st", [P, 2, ET, HPT, CH], BF16)
        v_t = sb("v_t", [P, 2, WPC, E])
        probs = sb("probs", [P, 2, HPT * W])
        o_sb = sb("o_sb", [P, ET, S])
        g_sb = xn
        maskbc = sb("maskbc", [P, S])
        neg_row = sb("neg_row", [1, 2, CH], BF16)
        maskt = sb("maskt", [P, S // W])
        key_bias = sb("key_bias", [P, S // W])
        wq = sb("wq", [P, 2, DT, E], BF16)
        wk = sb("wk", [P, 2, DT, E], BF16)
        wv = sb("wv", [P, 2, DT, E], BF16)
        wo = sb("wo", [P, 2, ET, D], BF16)
        w_raw = [xb[:, i // 2, i % 2 * (S // 2):(i % 2 + 1) * (S // 2)] for i in range(4)]
        wb = sb("wb", [P, C // P, C])
        wf = sb("wf", [P, SC, NL])
        bq_sb = sb("bq_sb", [P, ET])
        bk_sb = sb("bk_sb", [P, ET])
        bv_sb = sb("bv_sb", [P, ET])
        bo_sb = sb("bo_sb", [P, DT])
        base_sb = sb("base_sb", [P, NL])
        id_sb = sb("id_sb", [P, P])
        id_bf = sb("id_bf", [P, P], BF16)
        sti = sb("sti", [P, NL])
        eye_sb = sb("eye_sb", [P, N * N])
        eye_g = sb("eye_g", [P, N * N])
        gate_sb = sb("gate_sb", [P, 3])
        gt = sb("gt", [P, 8])
        ones = sb("ones", [P, P])
        spare = sb("spare", [P, 5])
        zero4 = sb("zero4", [P, HPT])
        csum = sb("csum", [P, NL])
        bn_a = sb("bn_a", [P, DT, 4, 6])
        mv_a = sb("mv_a", [P, DT, 2])
        ra = sb("ra", [P, 5, DT])
        negm = sb("negm", [P, 2, HPT])
        negm_hl = sb("negm_hl", [P, 2, 2, HPT], BF16)
        lnden = sb("lnden", [P, 2, P])
        rden = sb("rden", [P, 2, P])
        bn_b = sb("bn_b", [P, DT, 4, 6])
        mv_b = sb("mv_b", [P, DT, 2])
        rb = sb("rb", [P, 8, DT])
        xt_sb = sb("xt_sb", [P, 2, DT * P])
        wo_tmp = xt_sb
        logit = sb("logit", [P, DT, NL])
        soft = sb("soft", [P, DT, 2, N])
        smx = sb("smx", [P, DT * N])
        sln = sb("sln", [P, DT * N])
        zl = sb("zl", [P, DT, N, N])
        ke = sb("ke", [P, DT, N, N])
        kp = sb("kp", [P, DT, N, N])
        sa = sb("sa", [P, DT, N])
        sv = sb("sv", [P, DT, N])
        ssum = sb("ssum", [P, DT * N])
        cmat = sb("cmat", [P, DT, N, N])
        ccon = sb("ccon", [P, DT, N])
        pre = sb("pre", [P, DT, N])
        post = sb("post", [P, DT, N])
        xpre = xt_sb[:, 0]
        xpt = xt_sb[:, 1]
        lgs = xpt
        otile = sb("otile", [P, N, C])

        pr = [ps("pr0"), ps("pr1")]
        s_ps = ps("s_ps")
        st_ps = [ps("st0"), ps("st1")]
        av_ps = ps("av_ps")
        f0 = ps("f0")
        f1 = ps("f1")

        w_loaded = sem("w_loaded")
        x_loaded = [sem(f"x_loaded{t}") for t in range(DT)]
        ctx_loaded = sem("ctx_loaded")
        stack_loaded = [sem(f"stack_loaded{i}") for i in range(2)]
        negrow_ready = sem("negrow_ready")
        w_split = sem("w_split")
        ctx_hi = sem("ctx_hi")
        ctx_split = sem("ctx_split")
        x_norm = sem("x_norm")
        x_hi = sem("x_hi")
        x_split = sem("x_split")
        qk_hi = sem("qk_hi")
        parts_hi = sem("parts_hi")
        max_split = sem("max_split")
        gelu_hi = sem("gelu_hi")
        maskbc_loaded = sem("maskbc_loaded")
        maskt_loaded = sem("maskt_loaded")
        zeroed = sem("zeroed")
        consts_ready = sem("consts_ready")
        csum_full = sem("csum_full")
        gates_act = sem("gates_act")
        setup_done = sem("setup_done")
        var_ready = sem("var_ready")
        rs_act = sem("rs_act")
        xstat_ready = sem("xstat_ready")
        proj_full = sem("proj_full")
        qk_ready = sem("qk_ready")
        v_ready = sem("v_ready")
        wo_read = sem("wo_read")
        s_full = sem("s_full")
        max_done = sem("max_done")
        st_full = sem("st_full")
        exp_done = sem("exp_done")
        av_full = sem("av_full")
        ln_done = sem("ln_done")
        rden_done = sem("rden_done")
        o_done = sem("o_done")
        gelu_done = sem("gelu_done")
        x1_added = sem("x1_added")
        mask_ready = sem("mask_ready")
        t_full = sem("t_full")
        t_copied = sem("t_copied")
        lg_full = sem("lg_full")
        lg_copied = sem("lg_copied")
        sel_full = sem("sel_full")
        small_req = sem("small_req")
        small_done = sem("small_done")
        xp_first = sem("xp_first")
        xpre_ready = sem("xpre_ready")
        xt_full = sem("xt_full")
        xt_copied = sem("xt_copied")
        y_full = sem("y_full")
        coef_ready = sem("coef_ready")
        acc_ready = sem("acc_ready")
        out_ready = sem("out_ready")
        out_stored = [sem(f"out_stored{i}") for i in range(2)]
        dve_setup = sem("dve_setup")
        dve_att = sem("dve_att")
        dve_ffn = sem("dve_ffn")

        xr = x.rearrange("b (t p) s -> b t p s", p=P)
        cr = ctx4.rearrange("b (t p) s -> b p t s", p=P)
        outr = out.rearrange("b (t p) s -> b t p s", p=P)

        WEIGHTS = [
            *((dst.rearrange("p (t e) -> p t e", t=src.shape[0] // P), src.rearrange("(t p) e -> p t e", p=P))
              for dst, src in zip(w_raw, (wq_t, wk_t, wv_t, wo_t))),
            (wb[:], w_branch.rearrange("(t p) e -> p t e", p=P)), (wf[:], wf_t.rearrange("(t p) e -> p t e", p=P)),
            (bq_sb[:], bq), (bk_sb[:], bk), (bv_sb[:], bv), (bo_sb[:], bo), (base_sb[:], base),
            (id_sb[:], ident), (sti[:], stack_i), (eye_sb[:], eye4), (gate_sb[:], gates),
        ]

        SINK_STEP = 1
        SINK_PER_STEP = 3
        XPRE_STEPS = [17, 20, 23, 26]
        OUT_STEPS = [[19, 20], [22, 23], [25, 26], [28, 29]]
        STEPS = UNITS + 2

        block = ctx.enter_context(nc.Block())

        def o_part(et, w, m):
            both = o_sb[:, et, w * WO_COLS:(w + 1) * WO_COLS].bitcast(BF16)
            return both[:, m * WO_COLS:(m + 1) * WO_COLS]

        @block.sync
        def _(sp):
            for dst, src in WEIGHTS:
                sp.dma_start(dst, src).then_inc(w_loaded, 16)

            def load_x(b, t):
                sp.dma_start(xa[:, t, :], xr[bass.ds(b, 1), t].rearrange("o p s -> (o p) s")).then_inc(x_loaded[t], 16)

            def load_ctx(b, c):
                sp.dma_start(ctx_raw[:], cr[bass.ds(b, 1), :, :, c * CH:(c + 1) * CH]
                             .rearrange("o p t s -> (o p) t s")).then_inc(ctx_loaded, 16)

            def load_masks(b):
                sp.dma_start(maskbc[:], mask_bc[bass.ds(b, 1), :].broadcast_to([P, S])).then_inc(maskbc_loaded, 16)
                sp.dma_start(maskt[:], mask_t[bass.ds(b, 1)].rearrange("o p w -> (o p) w")).then_inc(maskt_loaded, 16)

            def stack(b, c, dst, blocks):
                for r, (src, part) in enumerate(blocks):
                    for h in range(HPT):
                        sp.dma_start(dst[r * DH:(r + 1) * DH, c % 2, :, h, :],
                                     src[h * DH:(h + 1) * DH, part, :, :]).then_inc(stack_loaded[c % 2], 16)

            def body(b, more):
                for c in range(NC):
                    sp.wait_ge(qk_ready, b * (4 * NC) + 4 * c + 2)
                    stack(b, c, q_st, ((q_hl, 0), (q_hl, 1), (q_hl, 0)))
                    sp.wait_ge(qk_ready, b * (4 * NC) + 4 * c + 4)
                    stack(b, c, k_st, ((k_hl, 0), (k_hl, 0), (k_hl, 1)))
                    sp.wait_ge(negrow_ready, b * NC + c + 1)
                    sp.dma_start(k_st[ROWS:ROWS + 1, c % 2].rearrange("p t h j -> p (t h) j"),
                                 bcast(neg_row[:, c % 2, :], 1, HEADS)).then_inc(stack_loaded[c % 2], 16)
                    if c < NC - 2:
                        sp.wait_ge(ctx_split, b * NC + c + 2)
                        load_ctx(b, c + 2)
                    if c == NC - 2 and more:
                        sp.wait_ge(ctx_split, b * NC + NC)
                        load_ctx(b + 1, 0)
                if more:
                    for t in range(DT):
                        sp.wait_ge(x1_added, b * (DT * NW) + NW * (t + 1))
                        load_x(b + 1, t)
                    sp.wait_ge(wo_read, (b + 1) * (DT * NW))
                    load_masks(b + 1)
                    sp.wait_ge(ctx_split, (b + 1) * NC + 1)
                    load_ctx(b + 1, 1)

            load_ctx(0, 0)
            for t in range(DT):
                load_x(0, t)
            load_masks(0)
            sp.wait_ge(ctx_split, 1)
            load_ctx(0, 1)
            body(0, True)
            with sp.Fori(1, B - 1) as b:
                body(b, True)
            body(B - 1, False)

        @block.gpsimd
        def _(pool):
            pool.memset(q_st[ROWS:ROWS + 1], 1.0).then_inc(zeroed, 1)
            pool.wait_ge(zeroed, 1)
            pool.memset(spare[:, 2:3], 0.0).then_inc(zeroed, 1)
            pool.wait_ge(zeroed, 2)

            def split_ctx(b, c):
                for t in range(DT):
                    pool.wait_ge(ctx_hi, b * (NC * DT) + c * DT + t + 1)
                    ins = nc.gpsimd.tensor_tensor(ctx_hl[:, 1, t, :], ctx_raw[:, t, :], ctx_hl[:, 0, t, :],
                                                  ALU.subtract)
                ins.then_inc(ctx_split, 1)

            def split_x(b, c, t, first=False):
                n = c * DT + t
                if n == 0:
                    pool.wait_ge(xstat_ready, b + 1)
                    nc.gpsimd.tensor_tensor(spare[:, 4:5], spare[:, 2:3], spare[:, 2:3], ALU.add)
                nc.gpsimd.tensor_scalar(xn[:, n % 2, :], xa[:, t, c * CH:(c + 1) * CH],
                                        ra[:, 2, t:t + 1], ra[:, 4, t:t + 1], ALU.mult, ALU.add
                                        ).then_inc(x_norm, 1)
                pool.wait_ge(x_norm, b * (NC * DT) + n + 1)
                pool.wait_ge(x_hi, b * (NC * DT) + n + 1)
                if not (first and n == 0):
                    pool.wait_ge(x_split, b * (NC * DT) + n)
                nc.gpsimd.tensor_tensor(x_hl[:, 1, t, :], xn[:, n % 2, :], x_hl[:, 0, t, :], ALU.subtract
                                        ).then_inc(x_split, 1)

            def split_max(b, u, first):
                pool.wait_ge(max_done, b * UNITS + u + 1)
                if not (first and u < 2):
                    pool.wait_ge(st_full, b * UNITS + u - 1)
                nc.gpsimd.tensor_tensor(negm_hl[:, u % 2, 0, :], negm[:, u % 2, :], zero4[:], ALU.add
                                        ).then_inc(parts_hi, 1)
                pool.wait_ge(parts_hi, b * UNITS + u + 1)
                nc.gpsimd.tensor_tensor(negm_hl[:, u % 2, 1, :], negm[:, u % 2, :], negm_hl[:, u % 2, 0, :],
                                        ALU.subtract).then_inc(max_split, 1)

            def add_attention(b, t, w):
                n = t * NW + w
                pool.wait_ge(wo_read, b * (DT * NW) + n + 1)
                nc.gpsimd.tensor_tensor(xb[:, t, w * WO_COLS:(w + 1) * WO_COLS],
                                        xa[:, t, w * WO_COLS:(w + 1) * WO_COLS],
                                        wo_tmp[:, n % 2, :], ALU.add).then_inc(x1_added, 1)

            def store(bf, t, pair):
                pool.wait_ge(out_ready, bf * (2 * DT) + 2 * t + pair + 1)
                half = slice(2 * pair * C, 2 * (pair + 1) * C)
                pool.dma_start(outr[bass.ds(bf, 1), t, :, half].rearrange("o p s -> (o p) s"),
                               otile[:, 2 * pair:2 * pair + 2, :].rearrange("p n c -> p (n c)")
                               ).then_inc(out_stored[pair], 16)

            def body(b, att, ffn, first=False):
                bf = b - 1
                if att:
                    split_ctx(b, 0)
                    for t in range(DT):
                        split_x(b, 0, t, first)
                    split_ctx(b, 1)
                    for t in range(DT):
                        split_x(b, 1, t)
                for k in range(STEPS):
                    if att:
                        if k < UNITS:
                            split_max(b, k, first)
                        c, r = divmod(k, UPC)
                        if c + 2 < NC:
                            if r >= 4:
                                split_x(b, c + 2, r - 4)
                            if r == 6:
                                split_ctx(b, c + 2)
                    if ffn:
                        for t in range(DT):
                            for pair in range(2):
                                if k == OUT_STEPS[t][pair]:
                                    store(bf, t, pair)
                if att:
                    for t in range(DT):
                        for w in range(NW):
                            add_attention(b, t, w)

            body(0, True, False, first=True)
            with pool.Fori(1, B) as b:
                body(b, True, True)
            body(B, False, True)
            for pair in range(2):
                pool.wait_ge(out_stored[pair], 16 * DT * B)

        @block.tensor
        def _(pe):
            def pr_free(b, n):
                if n < 2:
                    pe.wait_ge(wo_read, b * (DT * NW))
                elif n - 2 < PROJ:
                    kind, c, i = PROJ_USES[n - 2]
                    if kind == "v":
                        pe.wait_ge(v_ready, b * (2 * NC) + 2 * c + i + 1)
                    else:
                        pe.wait_ge(qk_ready, b * (4 * NC) + 4 * c + 2 * "qk".index(kind) + i + 1)
                else:
                    pe.wait_ge(wo_read, b * (DT * NW) + n - 2 - PROJ + 1)

            PARTS = ((0, 0), (0, 1), (1, 0))

            def project(b, kind, c, i, first):
                n = use(kind, c, i)
                if not (first and n < 2):
                    pr_free(b, n)
                bank = pr[n % 2]
                if kind in "qk":
                    if i == 0 and kind == "q":
                        pe.wait_ge(x_split, b * (NC * DT) + (c + 1) * DT)
                    w = {"q": wq, "k": wk}[kind]
                    for t in range(DT):
                        for a, m in PARTS:
                            ins = nc.tensor.matmul(bank[:], w[:, a, t, i * P:(i + 1) * P], x_hl[:, m, t, :],
                                                   start=(t == 0 and a + m == 0), stop=(t == DT - 1 and a == 1))
                else:
                    if i == 0:
                        pe.wait_ge(ctx_split, b * NC + c + 1)
                    for j in range(2):
                        win = slice((2 * i + j) * W, (2 * i + j + 1) * W)
                        for t in range(DT):
                            for a, m in PARTS:
                                ins = nc.tensor.matmul(bank[:, j * E:(j + 1) * E], ctx_hl[:, a, t, win],
                                                       wv[:, m, t, :],
                                                       start=(t == 0 and a + m == 0), stop=(t == DT - 1 and a == 1))
                ins.then_inc(proj_full, 1)

            def place(u):
                c, r = divmod(u, UPC)
                return c, r // ET, r % ET

            def scores(b, u, first):
                c, w, et = place(u)
                if u % UPC == 0:
                    pe.wait_ge(stack_loaded[c % 2], b * (STACKED * NC // 2) + STACKED * (c // 2 + 1))
                if not (first and u == 0):
                    pe.wait_ge(max_done, b * UNITS + u)
                win = slice(w * W, (w + 1) * W)
                for h in range(HPT):
                    ins = nc.tensor.matmul(s_ps[:, h * W:(h + 1) * W], q_st[0:ROWS + 1, c % 2, et, h, win],
                                           k_st[0:ROWS + 1, c % 2, et, h, win], start=True, stop=True)
                ins.then_inc(s_full, 1)

            def scores_t(b, u, first):
                c, w, et = place(u)
                if not (first and u < 2):
                    pe.wait_ge(exp_done, b * UNITS + u - 1)
                win = slice(w * W, (w + 1) * W)
                bank = st_ps[u % 2]
                pe.wait_ge(max_split, b * UNITS + u + 1)
                for h in range(HPT):
                    part = bank[:, h * W:(h + 1) * W]
                    nc.tensor.matmul(part, k_st[0:ROWS, c % 2, et, h, win], q_st[0:ROWS, c % 2, et, h, win],
                                     start=True, stop=False)
                    for m in range(2):
                        ins = nc.tensor.matmul(part, negm_hl[:, u % 2, m, h:h + 1].broadcast_to([P, P]), id_bf[:],
                                               start=False, stop=(m == 1))
                ins.then_inc(st_full, 1)

            def values(b, u, first):
                c, w, et = place(u)
                pe.wait_ge(exp_done, b * UNITS + u + 1)
                if u % UPC == 0:
                    pe.wait_ge(v_ready, b * (2 * NC) + 2 * c + 2)
                if not (first and u == 0):
                    pe.wait_ge(o_done, b * UNITS + u)
                for h in range(HPT):
                    rows = slice(h * DH, (h + 1) * DH)
                    nc.tensor.matmul(av_ps[rows, 0:W], v_t[:, c % 2, w, et * P + h * DH:et * P + (h + 1) * DH],
                                     probs[:, u % 2, h * W:(h + 1) * W], start=True, stop=True)
                for h in range(HPT):
                    rows = slice(h * DH, (h + 1) * DH)
                    ins = nc.tensor.matmul(av_ps[rows, W:2 * W], ones[:, 0:DH],
                                           probs[:, u % 2, h * W:(h + 1) * W], start=True, stop=True)
                ins.then_inc(av_full, 1)

            def output(b, t, w):
                n = PROJ + t * NW + w
                pr_free(b, n)
                if t == 0:
                    pe.wait_ge(gelu_done, b * (ET * NW) + ET * (w + 1))
                for et in range(ET):
                    for a, m in PARTS:
                        ins = nc.tensor.matmul(pr[n % 2][:], wo[:, a, et, t * P:(t + 1) * P], o_part(et, w, m),
                                               start=(et == 0 and a + m == 0), stop=(et == ET - 1 and a == 1))
                ins.then_inc(proj_full, 1)

            def transpose_x(bf, k):
                if k == 0:
                    pe.wait_ge(x1_added, (bf + 1) * (DT * NW))
                else:
                    pe.wait_ge(t_copied, bf * SC + k)
                for t in range(DT):
                    ins = nc.tensor.transpose(f0[:, t * P:(t + 1) * P], xb[:, t, k * P:(k + 1) * P], id_sb[:])
                ins.then_inc(t_full, 1)

            def logits(bf, k):
                pe.wait_ge(t_copied, bf * SC + k + 1)
                g = k % 4
                nc.tensor.matmul(f1[g * NL:(g + 1) * NL, :], wf[:, k, :], xt_sb[:, k % 2, :],
                                 start=(k < 4), stop=(k >= SC - 4)).then_inc(lg_full, 1)

            def select(bf):
                pe.wait_ge(lg_copied, bf + 1)
                pe.wait_ge(t_copied, (bf + 1) * SC)
                for t in range(DT):
                    ins = nc.tensor.matmul(f0[:, t * NL:(t + 1) * NL], lgs[:, t * P:(t + 1) * P], sti[:],
                                           start=True, stop=True)
                ins.then_inc(sel_full, 1)

            def transpose_pre(bf, t):
                pe.wait_ge(xpre_ready, bf * DT + t + 1)
                if t:
                    pe.wait_ge(xt_copied, bf * DT + t)
                for j in range(C // P):
                    ins = nc.tensor.transpose(f0[:, j * P:(j + 1) * P], xpre[:, j * P:(j + 1) * P], id_sb[:])
                ins.then_inc(xt_full, 1)

            def branch(bf, t):
                pe.wait_ge(xt_copied, bf * DT + t + 1)
                if t:
                    pe.wait_ge(out_ready, bf * (2 * DT) + 2 * t)
                for j in range(C // P):
                    ins = nc.tensor.matmul(f1[:], xpt[:, j * P:(j + 1) * P], wb[:, j, :],
                                           start=(j == 0), stop=(j == C // P - 1))
                ins.then_inc(y_full, 1)

            def body(b, att, ffn, first=False):
                bf = b - 1
                if att:
                    project(b, *FIRST_USES[0], first)
                    project(b, *FIRST_USES[1], first)
                if ffn:
                    for j in range(SC):
                        transpose_x(bf, j)
                        if j:
                            logits(bf, j - 1)
                    logits(bf, SC - 1)
                    select(bf)
                if att:
                    for i in range(2, 6):
                        project(b, *FIRST_USES[i], first)
                for k in range(STEPS):
                    if att:
                        if k < UNITS:
                            scores(b, k, first)
                        if 1 <= k <= UNITS:
                            scores_t(b, k - 1, first)
                        if k >= 2:
                            values(b, k - 2, first)
                        c, r = divmod(k, UPC)
                        if c + 1 < NC and r < 6:
                            project(b, *PROJ_USES[6 * (c + 1) + r], first)
                    if ffn and k - 1 in XPRE_STEPS:
                        transpose_pre(bf, XPRE_STEPS.index(k - 1))
                        branch(bf, XPRE_STEPS.index(k - 1))
                if att:
                    for t in range(DT):
                        for w in range(NW):
                            output(b, t, w)

            pe.wait_ge(w_loaded, 16 * len(WEIGHTS))
            pe.wait_ge(consts_ready, 2)
            for k in range(SC):
                ins = nc.tensor.matmul(f0[:, 0:NL], ones[:], wf[:, k, :], start=(k == 0), stop=(k == SC - 1))
            ins.then_inc(csum_full, 1)
            pe.wait_ge(setup_done, 2)
            pe.wait_ge(w_split, 5)
            pe.wait_ge(zeroed, 2)
            body(0, True, False, first=True)
            with pe.Fori(1, B) as b:
                body(b, True, True)
            body(B, False, True)

        @block.scalar
        def _(act):
            exp_k = (ke[:], zl[:], ACT.Exp, 1.0)
            ln_sum = (sln[:], ssum[:], ACT.Ln, 1.0)
            small_list = [(rb[:, 1, :], rb[:, 0, :], ACT.Ln, 1.0), (rb[:, 2, :], rb[:, 1, :], ACT.Exp, -0.5),
                          (rb[:, 1, :], rb[:, 4, :], ACT.Ln, 1.0), (rb[:, 2, :], rb[:, 1, :], ACT.Exp, -0.5),
                          (soft[:], soft[:], ACT.Exp, 1.0),
                          exp_k, ln_sum, exp_k, ln_sum, exp_k]
            a_t, v_t4 = (v[:].rearrange("p t i -> p (t i)") for v in (sa, sv))
            for _ in RETURNS:
                small_list += [(sln[:], v_t4, ACT.Ln, 1.0), (sln[:], a_t, ACT.Ln, 1.0), exp_k]
            small_at = {0: 10}
            for it in RETURNS:
                k = SINK_STEP + (it - 1) // SINK_PER_STEP
                small_at[k] = small_at.get(k, 0) + 3

            def hi_ctx(b, c):
                act.wait_ge(ctx_loaded, b * (16 * NC) + 16 * (c + 1))
                if c:
                    act.wait_ge(proj_full, b * USES + use("v", c - 1, 1) + 1)
                for t in range(DT):
                    nc.scalar.activation(ctx_hl[:, 0, t, :], ctx_raw[:, t, :], ACT.Copy).then_inc(ctx_hi, 1)

            def hi_x(b, c, t):
                if c == 0 and t == 0:
                    act.wait_ge(xstat_ready, b + 1)
                if c and t == 0:
                    act.wait_ge(proj_full, b * USES + use("k", c - 1, 1) + 1)
                nc.scalar.activation(x_hl[:, 0, t, :], xa[:, t, c * CH:(c + 1) * CH], ACT.Identity,
                                     bias=ra[:, 4, t:t + 1], scale=ra[:, 2, t:t + 1]).then_inc(x_hi, 1)

            def xstat(b):
                act.wait_ge(var_ready, b + 1)
                nc.scalar.activation(ra[:, 1, :], ra[:, 0, :], ACT.Ln).then_inc(rs_act, 1)
                act.wait_ge(rs_act, 2 * b + 1)
                nc.scalar.activation(ra[:, 3, :], ra[:, 1, :], ACT.Exp, scale=-0.5).then_inc(rs_act, 1)

            def read_qk(b, kind, c, i, first):
                n = use(kind, c, i)
                act.wait_ge(proj_full, b * USES + n + 1)
                if i == 0 and kind == "q" and not (first and c == 0):
                    last = c - 1 if c else NC - 1
                    turns = b if c else b - 1
                    act.wait_ge(stack_loaded[last % 2], turns * (STACKED * NC // 2) + STACKED * (last // 2 + 1))
                dst, bias = {"q": (q_hl, bq_sb), "k": (k_hl, bk_sb)}[kind]
                nc.scalar.activation(dst[:, 0, i, :], pr[n % 2][:], ACT.Identity, bias=bias[:, i:i + 1]
                                     ).then_inc(qk_hi, 1)

            def read_v(b, c, i, first):
                n = use("v", c, i)
                act.wait_ge(proj_full, b * USES + n + 1)
                if i == 0 and not (first and c < 2):
                    act.wait_ge(av_full, b * UNITS + UPC * (c - 1))
                nc.scalar.activation(v_t[:, c % 2, 2 * i:2 * i + 2, :].rearrange("p w e -> p (w e)"), pr[n % 2][:],
                                     ACT.Copy).then_inc(v_ready, 1)

            def read_use(b, kind, c, i, first):
                if kind == "v":
                    read_v(b, c, i, first)
                else:
                    read_qk(b, kind, c, i, first)

            def exp_scores(b, u, first):
                g = u // ET
                act.wait_ge(st_full, b * UNITS + u + 1)
                if not (first and u < 2):
                    act.wait_ge(av_full, b * UNITS + u - 1)
                nc.scalar.activation(probs[:, u % 2, :], st_ps[u % 2][:], ACT.Exp,
                                     bias=key_bias[:, g:g + 1], scale=SCALE).then_inc(exp_done, 1)

            def inverse_den(b, u, first):
                act.wait_ge(av_full, b * UNITS + u + 1)
                if not (first and u < 2):
                    act.wait_ge(o_done, b * UNITS + u - 1)
                nc.scalar.activation(lnden[:, u % 2, :], av_ps[:, W:2 * W], ACT.Ln).then_inc(ln_done, 1)
                act.wait_ge(ln_done, b * UNITS + u + 1)
                nc.scalar.activation(rden[:, u % 2, :], lnden[:, u % 2, :], ACT.Exp, scale=-1.0
                                     ).then_inc(rden_done, 1)

            def gelu(b):
                nc.scalar.preload_act_table_set("gelu_and_others")
                act.wait_ge(o_done, (b + 1) * UNITS)
                for w in range(NW):
                    for et in range(ET):
                        n = w * ET + et
                        if n >= 2:
                            act.wait_ge(gelu_done, b * (ET * NW) + n - 1)
                        nc.scalar.activation(g_sb[:, n % 2, :], o_sb[:, et, w * WO_COLS:(w + 1) * WO_COLS], ACT.Gelu,
                                             bias=bv_sb[:, et:et + 1]).then_inc(gelu_hi, 1)
                        act.wait_ge(gelu_hi, b * (2 * ET * NW) + 2 * n + 1)
                        nc.scalar.activation(o_part(et, w, 0), g_sb[:, n % 2, :], ACT.Copy).then_inc(gelu_hi, 1)
                nc.scalar.preload_act_table_set("natural_log_exp_and_others")

            def copy_t(bf, k):
                act.wait_ge(t_full, bf * SC + k + 1)
                if k >= 2:
                    act.wait_ge(lg_full, bf * SC + k - 1)
                nc.scalar.activation(xt_sb[:, k % 2, :], f0[:], ACT.Copy).then_inc(t_copied, 1)

            def copy_lg(bf):
                act.wait_ge(lg_full, (bf + 1) * SC)
                nc.scalar.activation(lgs[:], f1[:], ACT.Copy).then_inc(lg_copied, 1)

            small = [0]

            def small_step(bf, dst, src, func, scale=1.0):
                small[0] += 1
                act.wait_ge(small_req, bf * SMALL + small[0])
                nc.scalar.activation(dst, src, func, scale=scale).then_inc(small_done, 1)

            def first_products(bf, t):
                if t == 0:
                    act.wait_ge(coef_ready, 2 * bf + 1)
                else:
                    act.wait_ge(xt_full, bf * DT + t)
                nc.scalar.activation(xpre[:], xb[:, t, 0:C], ACT.Identity, bias=rb[:, 6, t:t + 1],
                                     scale=pre[:, t, 0:1]).then_inc(xp_first, 1)

            def copy_pre(bf, t):
                act.wait_ge(xt_full, bf * DT + t + 1)
                if t:
                    act.wait_ge(y_full, bf * DT + t)
                nc.scalar.activation(xpt[:], f0[:], ACT.Copy).then_inc(xt_copied, 1)

            def first_out(bf, t, pair):
                if t == 0 and pair == 0:
                    act.wait_ge(coef_ready, 2 * bf + 2)
                if t:
                    act.wait_ge(out_stored[pair], 16 * (bf * DT + t))
                for i in range(2 * pair, 2 * pair + 2):
                    nc.scalar.activation(otile[:, i, :], xb[:, t, 0:C], ACT.Identity, bias=ccon[:, t, i:i + 1],
                                         scale=cmat[:, t, i, 0:1]).then_inc(acc_ready, 1)

            def small_steps(bf, n):
                for _ in range(n):
                    small_step(bf, *small_list[small[0]])

            def body(b, att, ffn, first=False):
                bf = b - 1
                small[0] = 0
                if att:
                    hi_ctx(b, 0)
                    read_use(b, *FIRST_USES[0], first)
                    read_use(b, *FIRST_USES[1], first)
                if ffn:
                    for j in range(SC):
                        copy_t(bf, j)
                    copy_lg(bf)
                if att:
                    xstat(b)
                    for t in range(DT):
                        hi_x(b, 0, t)
                    hi_ctx(b, 1)
                    for i in range(2, 6):
                        read_use(b, *FIRST_USES[i], first)
                    for t in range(DT):
                        hi_x(b, 1, t)
                for k in range(STEPS):
                    if att:
                        if 1 <= k <= UNITS:
                            exp_scores(b, k - 1, first)
                        if k >= 2:
                            inverse_den(b, k - 2, first)
                        c, r = divmod(k, UPC)
                        if c + 1 < NC and r < 6:
                            read_use(b, *PROJ_USES[6 * (c + 1) + r], first)
                        if c + 2 < NC:
                            if r >= 4:
                                hi_x(b, c + 2, r - 4)
                            if r == 6:
                                hi_ctx(b, c + 2)
                    if ffn:
                        if k in small_at:
                            small_steps(bf, small_at[k])
                        if k in XPRE_STEPS:
                            first_products(bf, XPRE_STEPS.index(k))
                        if k - 1 in XPRE_STEPS:
                            copy_pre(bf, XPRE_STEPS.index(k - 1))
                        for t in range(DT):
                            for pair in range(2):
                                if k == OUT_STEPS[t][pair]:
                                    first_out(bf, t, pair)
                if ffn:
                    assert small[0] == SMALL
                if att:
                    gelu(b)
                if ffn:
                    for pair in range(2):
                        act.wait_ge(out_stored[pair], (bf + 1) * (16 * DT))

            act.wait_ge(w_loaded, 16 * len(WEIGHTS))
            nc.scalar.activation(gt[:, 0:2], gate_sb[:, 0:2], ACT.Tanh).then_inc(gates_act, 1)
            nc.scalar.activation(gt[:, 4:5], gate_sb[:, 2:3], ACT.Exp, scale=-1.0).then_inc(gates_act, 1)
            act.wait_ge(setup_done, 1)
            for dst, src in zip((wq, wk, wv, wo), w_raw):
                nc.scalar.activation(dst[:, 0].rearrange("p t e -> p (t e)"), src, ACT.Copy).then_inc(w_split, 1)
            nc.scalar.activation(id_bf[:], id_sb[:], ACT.Copy).then_inc(w_split, 1)
            nc.scalar.preload_act_table_set("natural_log_exp_and_others")
            body(0, True, False, first=True)
            with act.Fori(1, B) as b:
                body(b, True, True)
            body(B, False, True)

        @block.vector
        def _(dve):
            setup = Chain(dve, dve_setup, 7)
            ca = Chain(dve, dve_att, DVE_ATT)
            cf = Chain(dve, dve_ffn, DVE_FFN)

            def newton(chain, r, guess, value, work):
                chain.link(nc.vector.tensor_tensor(work, guess, guess, ALU.mult))
                chain.link(nc.vector.tensor_tensor(work, work, value, ALU.mult))
                chain.link(nc.vector.tensor_scalar(work, work, -0.5, 1.5, ALU.mult, ALU.add))
                chain.link(nc.vector.tensor_tensor(r, guess, work, ALU.mult))

            def xstat(b):
                for t in range(DT):
                    dve.wait_ge(x_loaded[t], 16 * b + 16)
                    for j in range(4):
                        ins = nc.vector.bn_stats(bn_a[:, t, j, :], xa[:, t, j * 512:(j + 1) * 512])
                ca.link(ins)
                nc.vector.memset(spare[:, 0:1], 0.0)
                for t in range(DT):
                    ins = nc.vector.bn_aggr(mv_a[:, t, :], bn_a[:, t].rearrange("p j s -> p (j s)"))
                ca.link(ins)
                nc.vector.tensor_scalar(ra[:, 0, :], mv_a[:, :, 1], LN_EPS, None, ALU.add).then_inc(var_ready, 1)
                dve.wait_ge(maskbc_loaded, 16 * b + 16)
                dve.wait_ge(maskt_loaded, 16 * b + 16)
                nc.vector.tensor_scalar(key_bias[:], maskt[:], 0.0, NEG * SCALE, ALU.is_le, ALU.mult
                                        ).then_inc(mask_ready, 1)
                dve.wait_ge(rs_act, 2 * b + 2)
                newton(ca, ra[:, 2, :], ra[:, 3, :], ra[:, 0, :], ra[:, 1, :])
                nc.vector.scalar_tensor_tensor(out=ra[:, 4, :], in0=mv_a[:, :, 0], scalar=-1.0, in1=ra[:, 2, :],
                                               op0=ALU.mult, op1=ALU.mult).then_inc(xstat_ready, 1)

            def low_qk(b, kind, c, i, first):
                n = use(kind, c, i)
                m = 4 * c + 2 * "qk".index(kind) + i
                dve.wait_ge(qk_hi, b * (4 * NC) + m + 1)
                dst, bias = {"q": (q_hl, bq_sb), "k": (k_hl, bk_sb)}[kind]
                nc.vector.scalar_tensor_tensor(out=dst[:, 1, i, :], in0=pr[n % 2][:], scalar=bias[:, i:i + 1],
                                               in1=dst[:, 0, i, :], op0=ALU.add, op1=ALU.subtract
                                               ).then_inc(qk_ready, 1)
                if m % 4 == 3:
                    nc.vector.tensor_scalar(neg_row[:, c % 2, :], maskbc[0:1, c * CH:(c + 1) * CH], 0.0, NEG,
                                            ALU.is_le, ALU.mult).then_inc(negrow_ready, 1)

            def maximum(b, u, first):
                dve.wait_ge(s_full, b * UNITS + u + 1)
                if not (first and u < 2):
                    dve.wait_ge(max_split, b * UNITS + u - 1)
                nc.vector.tensor_reduce(negm[:, u % 2, :], s_ps[:].rearrange("p (h j) -> p h j", h=HPT),
                                        AX.X, ALU.max, negate=True).then_inc(max_done, 1)

            def divide(b, u, first):
                g, et = divmod(u, ET)
                dve.wait_ge(rden_done, b * UNITS + u + 1)
                if u == 0 and not first:
                    dve.wait_ge(proj_full, b * USES)
                nc.vector.tensor_tensor(o_sb[:, et, g * W:(g + 1) * W], av_ps[:, 0:W], rden[:, u % 2, :], ALU.mult
                                        ).then_inc(o_done, 1)

            def read_wo(b, t, w, first):
                n = t * NW + w
                dve.wait_ge(proj_full, b * USES + PROJ + n + 1)
                if not (first and n < 2):
                    dve.wait_ge(x1_added, b * (DT * NW) + n - 1)
                nc.vector.scalar_tensor_tensor(out=wo_tmp[:, n % 2, :], in0=pr[(PROJ + n) % 2][:],
                                               scalar=bo_sb[:, t:t + 1], in1=maskbc[:, w * WO_COLS:(w + 1) * WO_COLS],
                                               op0=ALU.add, op1=ALU.mult).then_inc(wo_read, 1)

            small = [0]

            def ask(bf, ins):
                small[0] += 1
                ins.then_inc(small_req, 1)
                dve.wait_ge(small_done, bf * SMALL + small[0])

            def stat_b(bf, t):
                if t == 0:
                    dve.wait_ge(x1_added, (bf + 1) * (DT * NW))
                for j in range(4):
                    ins = nc.vector.bn_stats(bn_b[:, t, j, :], xb[:, t, j * 512:(j + 1) * 512])
                cf.link(ins)
                nc.vector.memset(spare[:, 0:1], 0.0)
                cf.link(nc.vector.bn_aggr(mv_b[:, t, :], bn_b[:, t].rearrange("p j s -> p (j s)")))

            def stat_finish(bf):
                ask(bf, nc.vector.tensor_scalar(rb[:, 0, :], mv_b[:, :, 1], LN_EPS, None, ALU.add))
                ask(bf, nc.vector.tensor_scalar(rb[:, 7, :], mv_b[:, :, 0], -1.0, None, ALU.mult))
                newton(cf, rb[:, 3, :], rb[:, 2, :], rb[:, 0, :], rb[:, 1, :])
                cf.link(nc.vector.tensor_tensor(rb[:, 4, :], rb[:, 3, :], rb[:, 3, :], ALU.mult))
                cf.link(nc.vector.tensor_tensor(rb[:, 4, :], rb[:, 4, :], mv_b[:, :, 1], ALU.mult))
                ask(bf, nc.vector.tensor_scalar(rb[:, 4, :], rb[:, 4, :], RMS_EPS, None, ALU.add))
                ask(bf, nc.vector.tensor_tensor(rb[:, 6, :], rb[:, 7, :], rb[:, 3, :], ALU.mult))
                newton(cf, rb[:, 5, :], rb[:, 2, :], rb[:, 4, :], rb[:, 1, :])
                cf.link(nc.vector.tensor_tensor(rb[:, 5, :], rb[:, 5, :], rb[:, 3, :], ALU.mult))

            l_t = sln[:].rearrange("p (t i) -> p t i", t=DT)
            kcol = ke[:].rearrange("p t i j -> p t j i")
            zcol = zl[:].rearrange("p t i j -> p t j i")
            s_t = ssum[:].rearrange("p (t i) -> p t i", t=DT)
            m_t = smx[:].rearrange("p (t i) -> p t i", t=DT)

            def over_j(v):
                return bcast(v, 3, N)

            def over_i(v):
                return bcast(v, 2, N)

            def logits_and_softmax(bf):
                dve.wait_ge(sel_full, bf + 1)
                for t in range(DT):
                    ins = nc.vector.scalar_tensor_tensor(out=logit[:, t, :], in0=csum[:], scalar=rb[:, 7, t:t + 1],
                                                         in1=f0[:, t * NL:(t + 1) * NL], op0=ALU.mult, op1=ALU.add)
                cf.link(ins)
                for t in range(DT):
                    ins = nc.vector.scalar_tensor_tensor(out=logit[:, t, :], in0=logit[:, t, :],
                                                         scalar=rb[:, 5, t:t + 1], in1=base_sb[:],
                                                         op0=ALU.mult, op1=ALU.add)
                cf.link(ins)
                lpp = logit[:, :, N * N:N * N + 2 * N].rearrange("p t (k n) -> p t k n", k=2)
                m8 = kp[:].rearrange("p t i j -> p (t i j)")[:, 0:2 * DT].rearrange("p (t k) -> p t k", t=DT)
                cf.link(nc.vector.tensor_reduce(m8, lpp, AX.X, ALU.max))
                ask(bf, nc.vector.tensor_tensor(soft[:], lpp, bcast(m8, 3, N), ALU.subtract))
                cf.link(nc.vector.tensor_reduce(m8, soft[:], AX.X, ALU.add))
                cf.link(nc.vector.reciprocal(m8, m8))
                cf.link(nc.vector.tensor_tensor(soft[:], soft[:], bcast(m8, 3, N), ALU.mult))
                nc.vector.tensor_tensor(pre[:], soft[:, :, 0, :], bcast(rb[:, 3, :], 2, N), ALU.mult
                                        ).then_inc(coef_ready, 1)
                cf.link(nc.vector.tensor_scalar(post[:], soft[:, :, 1, :], gt[:, 1:2], None, ALU.mult))
                cf.link(nc.vector.tensor_scalar(zl[:].rearrange("p t i j -> p t (i j)"), logit[:, :, 0:N * N],
                                                1.0 / TAU, None, ALU.mult))
                for z, e in ((zl[:], ke[:]), (zcol, kcol)):
                    cf.link(nc.vector.tensor_reduce(m_t, z, AX.X, ALU.max))
                    ask(bf, nc.vector.tensor_tensor(z, z, bcast(m_t, 3, N), ALU.subtract))
                    ask(bf, nc.vector.tensor_reduce(s_t, e, AX.X, ALU.add))
                    less = nc.vector.tensor_tensor(z, z, bcast(l_t, 3, N), ALU.subtract)
                    if e is kcol:
                        ask(bf, less)
                    else:
                        cf.link(less)

            def sinkhorn(bf, it):
                kpc = kp[:].rearrange("p t i j -> p t j i")
                if it % SEG == 1:
                    cf.link(nc.vector.tensor_reduce(s_t, ke[:], AX.X, ALU.add))
                else:
                    cf.link(nc.vector.tensor_tensor(kp[:], ke[:], over_i(sv[:]), ALU.mult))
                    cf.link(nc.vector.tensor_reduce(s_t, kp[:], AX.X, ALU.add))
                cf.link(nc.vector.reciprocal(sa[:], s_t))
                cf.link(nc.vector.tensor_tensor(kp[:], ke[:], over_j(sa[:]), ALU.mult))
                cf.link(nc.vector.tensor_reduce(s_t, kpc, AX.X, ALU.add))
                made = nc.vector.reciprocal(sv[:], s_t)
                if it % SEG or it == ITERS - 1:
                    cf.link(made)
                else:
                    ask(bf, made)
                    ask(bf, nc.vector.tensor_tensor(zl[:], zl[:], over_i(l_t), ALU.add))
                    ask(bf, nc.vector.tensor_tensor(zl[:], zl[:], over_j(l_t), ALU.add))

            def coefficients(bf):
                cf.link(nc.vector.tensor_tensor(kp[:], ke[:], over_j(sa[:]), ALU.mult))
                cf.link(nc.vector.tensor_tensor(kp[:], kp[:], over_i(sv[:]), ALU.mult))
                flat = kp[:].rearrange("p t i j -> p t (i j)")
                cf.link(nc.vector.tensor_scalar(flat, flat, gt[:, 2:3], None, ALU.mult))
                cf.link(nc.vector.tensor_tensor(flat, flat, bcast(eye_g[:], 1, DT), ALU.add))
                cf.link(nc.vector.tensor_scalar(flat, flat, gt[:, 1:2], None, ALU.mult))
                cf.link(nc.vector.tensor_reduce(s_t, kp[:], AX.X, ALU.add))
                cf.link(nc.vector.tensor_tensor(ccon[:], s_t, bcast(rb[:, 6, :], 2, N), ALU.mult))
                cf.link(nc.vector.tensor_tensor(flat, flat, bcast(rb[:, 3, :], 2, N * N), ALU.mult))
                nc.vector.tensor_tensor(cmat[:].rearrange("p t i j -> p t (i j)"), flat, bcast(eye_sb[:], 1, DT),
                                        ALU.add).then_inc(coef_ready, 1)
                dve.wait_ge(coef_ready, 2 * bf + 2)

            def make_xpre(bf, t):
                dve.wait_ge(xp_first, bf * DT + t + 1)
                for n in range(1, N):
                    ins = nc.vector.scalar_tensor_tensor(out=xpre[:], in0=xb[:, t, n * C:(n + 1) * C],
                                                         scalar=pre[:, t, n:n + 1], in1=xpre[:],
                                                         op0=ALU.mult, op1=ALU.add)
                    if n < N - 1:
                        cf.link(ins)
                ins.then_inc(xpre_ready, 1)

            def make_out(bf, t, pair):
                streams = range(2 * pair, 2 * pair + 2)
                for j in range(1, N):
                    for i in streams:
                        if j == 1:
                            dve.wait_ge(acc_ready, bf * (DT * N) + t * N + i + 1)
                        ins = nc.vector.scalar_tensor_tensor(out=otile[:, i, :], in0=xb[:, t, j * C:(j + 1) * C],
                                                             scalar=cmat[:, t, i, j:j + 1], in1=otile[:, i, :],
                                                             op0=ALU.mult, op1=ALU.add)
                    cf.link(ins)
                if pair == 0:
                    dve.wait_ge(y_full, bf * DT + t + 1)
                for i in streams:
                    ins = nc.vector.scalar_tensor_tensor(out=otile[:, i, :], in0=f1[:], scalar=post[:, t, i:i + 1],
                                                         in1=otile[:, i, :], op0=ALU.mult, op1=ALU.add)
                ins.then_inc(out_ready, 1)

            def low_gelu(b, w, et):
                n = w * ET + et
                dve.wait_ge(gelu_hi, b * (2 * ET * NW) + 2 * n + 2)
                nc.vector.tensor_tensor(o_part(et, w, 1), g_sb[:, n % 2, :], o_part(et, w, 0), ALU.subtract
                                        ).then_inc(gelu_done, 1)

            def body(b, att, ffn, first=False):
                bf = b - 1
                small[0] = 0
                if ffn:
                    cf.start(bf)
                    for t in range(DT):
                        stat_b(bf, t)
                if att:
                    ca.start(b)
                    xstat(b)
                    for i in range(2, 6):
                        low_qk(b, *FIRST_USES[i], first)
                for k in range(STEPS):
                    if att:
                        if k < UNITS:
                            maximum(b, k, first)
                        if k >= 2:
                            divide(b, k - 2, first)
                        c, r = divmod(k, UPC)
                        if c + 1 < NC and r < 4:
                            low_qk(b, *PROJ_USES[6 * (c + 1) + r], first)
                    if ffn:
                        if k == 0:
                            stat_finish(bf)
                            logits_and_softmax(bf)
                        if k >= SINK_STEP:
                            i0 = 1 + SINK_PER_STEP * (k - SINK_STEP)
                            for it in range(i0, min(i0 + SINK_PER_STEP, ITERS)):
                                sinkhorn(bf, it)
                            if i0 < ITERS <= i0 + SINK_PER_STEP:
                                coefficients(bf)
                        if k in XPRE_STEPS:
                            make_xpre(bf, XPRE_STEPS.index(k))
                        for t in range(DT):
                            for pair in range(2):
                                if k == OUT_STEPS[t][pair]:
                                    make_out(bf, t, pair)
                if ffn:
                    cf.end()
                if att:
                    for w in range(NW):
                        for et in range(ET):
                            low_gelu(b, w, et)
                    for t in range(DT):
                        for w in range(NW):
                            read_wo(b, t, w, first)
                    ca.end()

            nc.vector.memset(ones[:], 1.0).then_inc(consts_ready, 1)
            nc.vector.memset(zero4[:], 0.0).then_inc(consts_ready, 1)
            dve.wait_ge(w_loaded, 16 * len(WEIGHTS))
            dve.wait_ge(csum_full, 1)
            setup.link(nc.vector.tensor_copy(csum[:], f0[:, 0:NL]))
            dve.wait_ge(gates_act, 2)
            setup.link(nc.vector.tensor_scalar(gt[:, 5:6], gt[:, 4:5], 1.0, None, ALU.add))
            setup.link(nc.vector.reciprocal(gt[:, 2:3], gt[:, 5:6]))
            setup.link(nc.vector.tensor_scalar(gt[:, 3:4], gt[:, 2:3], -1.0, 1.0, ALU.mult, ALU.add))
            setup.link(nc.vector.tensor_scalar(eye_g[:], eye_sb[:], gt[:, 3:4], None, ALU.mult))
            setup.link(nc.vector.tensor_scalar(w_raw[3], w_raw[3], gt[:, 0:1], None, ALU.mult))
            setup.link(nc.vector.tensor_scalar(bo_sb[:], bo_sb[:], gt[:, 0:1], None, ALU.mult))
            setup.end()
            nc.vector.memset(spare[:, 0:1], 0.0).then_inc(setup_done, 1)
            for n, (dst, src) in enumerate(zip((wq, wk, wv, wo), w_raw)):
                dve.wait_ge(w_split, n + 1)
                ins = nc.vector.tensor_tensor(dst[:, 1].rearrange("p t e -> p (t e)"), src,
                                              dst[:, 0].rearrange("p t e -> p (t e)"), ALU.subtract)
            ins.then_inc(setup_done, 1)
            body(0, True, False, first=True)
            with dve.Fori(1, B) as b:
                body(b, True, True)
            body(B, False, True)


_OUTS = [((B, D, S), "float32")]


def kernel(x, ctx_4096, mask_Bx1x4096_ff1, g_xattn, g_ffn, L0_xattn_Wq, L0_xattn_bq, L0_xattn_Wk, L0_xattn_bk,
           L0_xattn_Wv, L0_xattn_bv, L0_xattn_Wo, L0_xattn_bo, L0_ffn_W_res, L0_ffn_W_pre, L0_ffn_W_post,
           L0_ffn_H_res_base, L0_ffn_H_pre_base, L0_ffn_H_post_base, L0_ffn_gate, L0_ffn_W_branch):
    import numpy as np
    import concourse.bacc as _bacc
    from concourse import mybir as _mybir
    from concourse.bass_utils import run_bass_kernel_spmd as _run

    A = np.asarray

    def rows(v):
        return np.broadcast_to(A(v).reshape(1, -1), (P, A(v).size))

    mask = A(mask_Bx1x4096_ff1)[:, 0, :]
    pad = np.zeros((NL - N * N - 2 * N, S), np.float32)
    ordered = [
        A(x), A(ctx_4096), mask, mask.reshape(B, S // W, W).transpose(0, 2, 1),
        np.concatenate([rows(g_xattn), rows(g_ffn), rows(L0_ffn_gate)], axis=1),
        A(L0_xattn_Wq).T, A(L0_xattn_bq).reshape(ET, P).T, A(L0_xattn_Wk).T, A(L0_xattn_bk).reshape(ET, P).T,
        A(L0_xattn_Wv).T, A(L0_xattn_bv).reshape(ET, P).T, A(L0_xattn_Wo).T, A(L0_xattn_bo).reshape(DT, P).T,
        np.concatenate([A(L0_ffn_W_res), A(L0_ffn_W_pre), A(L0_ffn_W_post), pad], axis=0).T,
        np.concatenate([rows(L0_ffn_H_res_base), rows(L0_ffn_H_pre_base), rows(L0_ffn_H_post_base),
                        np.zeros((P, NL - N * N - 2 * N), np.float32)], axis=1),
        A(L0_ffn_W_branch), np.eye(P, dtype=np.float32), np.tile(np.eye(NL, dtype=np.float32), (4, 1)),
        rows(np.eye(N, dtype=np.float32)),
    ]
    nc = _bacc.Bacc("TRN2", target_bir_lowering=False, num_devices=1, dynamic_dma_scratch_size=4096)
    arrays, args = {}, []
    for i, a in enumerate(ordered):
        a = np.ascontiguousarray(a)
        arrays[f"in_{i}_dram"] = a
        args.append(nc.dram_tensor(f"in_{i}_dram", a.shape, _mybir.dt.from_np(a.dtype), kind="ExternalInput").ap())
    for i, (shape, dtype) in enumerate(_OUTS):
        dt = _mybir.dt.from_np(np.dtype(dtype))
        args.append(nc.dram_tensor(f"out_{i}_dram", shape, dt, kind="ExternalOutput").ap())
    program(nc, *args)
    r = _run(nc, [arrays], core_ids=[0])
    return tuple(r.results[0][f"out_{i}_dram"] for i in range(len(_OUTS)))[0]
```

```python
from contextlib import ExitStack

import concourse.bass as bass
from concourse import mybir

F32 = mybir.dt.float32
BF16 = mybir.dt.bfloat16
ALU = mybir.AluOpType
ACT = mybir.ActivationFunctionType
AX = mybir.AxisListType

P = 128
B, D, S = 8, 512, 2048
W = 128
HEADS, DH = 8, 32
E = HEADS * DH
DT = D // P
ET = E // P
HPT = P // DH
CH = 4 * W
NC = S // CH
WPC = CH // W
UNITS = S // W * ET
UPC = UNITS // NC
WO_COLS = 512
NW = S // WO_COLS
SCALE = float(DH) ** -0.5
NEG = -float(2 ** 40)
LN_EPS = 1e-5
RMS_EPS = 1.1920929e-07
N = 4
C = S // N
NL = 32
ITERS = 50
TAU = 0.1
SEG = 10

FIRST_USES = [("v", 0, 0), ("v", 0, 1), ("q", 0, 0), ("q", 0, 1), ("k", 0, 0), ("k", 0, 1)]
PROJ_USES = list(FIRST_USES)
for _c in range(NC + 1):
    if _c + 1 < NC:
        PROJ_USES += [(kind, _c + 1, i) for kind in "qkv" for i in range(2)]
    if _c:
        PROJ_USES += [("o", _c - 1, t) for t in range(DT)]
USES = len(PROJ_USES)
OUTPUT_AT = 6
GELU_AT = 2
ROWS = 3 * DH
STACK_DMAS = 6 * HPT + 1
STACKED = 16 * STACK_DMAS
SC = S // P
RETURNS = range(SEG, ITERS, SEG)
SMALL = 10 + 3 * len(RETURNS)
DVE_ATT = 6
DVE_FFN = 355


def use(kind, c, i):
    return PROJ_USES.index((kind, c, i))


def uses_at(c):
    return [(kind, c + 1, i) for kind in "qkv" for i in range(2)]


def bcast(ap, axis, n):
    ap = ap.unsqueeze(axis)
    shape = list(ap.shape)
    shape[axis] = n
    return ap.broadcast_to(shape)


class Chain:

    def __init__(self, eng, sem, per_batch):
        self.eng, self.sem, self.per, self.n, self.base = eng, sem, per_batch, 0, 0

    def start(self, b):
        self.n, self.base = 0, b * self.per

    def link(self, ins):
        self.n += 1
        ins.then_inc(self.sem, 1)
        self.eng.wait_ge(self.sem, self.base + self.n)

    def end(self):
        assert self.n == self.per, (self.n, self.per)


def program(nc, x, ctx4, mask_bc, mask_t, gates, wq_t, bq, wk_t, bk, wv_t, bv, wo_t, bo, wf_t, base,
            w_branch, ident, stack_i, eye4, out):
    with ExitStack() as ctx:
        def sb(name, shape, dt=F32):
            return ctx.enter_context(nc.sbuf_tensor(name, shape, dt))

        def ps(name):
            return ctx.enter_context(nc.psum_tensor(name, [P, 512], F32))

        def sem(name):
            return ctx.enter_context(nc.semaphore(name))

        x2 = [sb("x_even", [P, DT, S]), sb("x_odd", [P, DT, S])]
        ctx_raw = sb("ctx_raw", [P, DT, CH])
        ctx_hl = sb("ctx_hl", [P, 2, DT, CH], BF16)
        x_hl = sb("x_hl", [P, 2, DT, CH], BF16)
        xn = sb("xn", [P, 2, CH])
        q_hl = sb("q_hl", [P, 2, ET, CH], BF16)
        k_hl = sb("k_hl", [P, 2, ET, CH], BF16)
        q_st = sb("q_st", [P, 2, ET, HPT, CH], BF16)
        k_st = sb("k_st", [P, 2, ET, HPT, CH], BF16)
        v_t = sb("v_t", [P, 2, WPC, E])
        probs = sb("probs", [P, 2, HPT * W])
        o_sb = sb("o_sb", [P, 2, ET, CH])
        g_sb = sb("g_sb", [P, 2, WO_COLS])
        maskbc = sb("maskbc", [P, S])
        neg_row = sb("neg_row", [1, 2, CH], BF16)
        maskt = sb("maskt", [P, S // W])
        key_bias = sb("key_bias", [P, S // W])
        wq = sb("wq", [P, 2, DT, E], BF16)
        wk = sb("wk", [P, 2, DT, E], BF16)
        wv = sb("wv", [P, 2, DT, E], BF16)
        wo = sb("wo", [P, 2, ET, D], BF16)
        w_raw = [x2[1][:, i // 2, i % 2 * (S // 2):(i % 2 + 1) * (S // 2)] for i in range(4)]
        wb = sb("wb", [P, C // P, C])
        wf = sb("wf", [P, SC, NL])
        bq_sb = sb("bq_sb", [P, ET])
        bk_sb = sb("bk_sb", [P, ET])
        bv_sb = sb("bv_sb", [P, ET])
        bo_sb = sb("bo_sb", [P, DT])
        base_sb = sb("base_sb", [P, NL])
        id_sb = sb("id_sb", [P, P])
        id_bf = sb("id_bf", [P, P], BF16)
        sti = sb("sti", [P, NL])
        eye_sb = sb("eye_sb", [P, N * N])
        eye_g = sb("eye_g", [P, N * N])
        gate_sb = sb("gate_sb", [P, 3])
        gt = sb("gt", [P, 8])
        ones = sb("ones", [P, P])
        spare = sb("spare", [P, 5])
        zero4 = sb("zero4", [P, HPT])
        csum = sb("csum", [P, NL])
        bn_a = sb("bn_a", [P, DT, 4, 6])
        mv_a = sb("mv_a", [P, DT, 2])
        ra = sb("ra", [P, 5, DT])
        negm = sb("negm", [P, 2, HPT])
        negm_hl = sb("negm_hl", [P, 2, 2, HPT], BF16)
        lnden = sb("lnden", [P, 2, P])
        rden = sb("rden", [P, 2, P])
        bn_b = sb("bn_b", [P, DT, 4, 6])
        mv_b = sb("mv_b", [P, DT, 2])
        rb = sb("rb", [P, 8, DT])
        xt_sb = sb("xt_sb", [P, 2, DT * P])
        wo_tmp = sb("wo_tmp", [P, 2, WO_COLS])
        logit = sb("logit", [P, DT, NL])
        soft = sb("soft", [P, DT, 2, N])
        smx = sb("smx", [P, DT * N])
        sln = sb("sln", [P, DT * N])
        zl = sb("zl", [P, DT, N, N])
        ke = sb("ke", [P, DT, N, N])
        kp = sb("kp", [P, DT, N, N])
        sa = sb("sa", [P, DT, N])
        sv = sb("sv", [P, DT, N])
        ssum = sb("ssum", [P, DT * N])
        cmat = sb("cmat", [P, DT, N, N])
        ccon = sb("ccon", [P, DT, N])
        pre = sb("pre", [P, DT, N])
        post = sb("post", [P, DT, N])
        xpre = xt_sb[:, 0]
        xpt = xt_sb[:, 1]
        lgs = xpt
        otile = sb("otile", [P, N, C])

        pr = [ps("pr0"), ps("pr1")]
        s_ps = ps("s_ps")
        st_ps = [ps("st0"), ps("st1")]
        av_ps = ps("av_ps")
        f0 = ps("f0")
        f1 = ps("f1")
        t_ps = [f0, s_ps]

        w_loaded = sem("w_loaded")
        x_loaded = [sem(f"x_loaded{t}") for t in range(DT)]
        ctx_loaded = sem("ctx_loaded")
        stack_loaded = [sem(f"stack_loaded{i}") for i in range(2)]
        negrow_ready = sem("negrow_ready")
        w_split = sem("w_split")
        ctx_hi = sem("ctx_hi")
        ctx_split = sem("ctx_split")
        x_norm = sem("x_norm")
        x_hi = sem("x_hi")
        x_split = sem("x_split")
        qk_hi = sem("qk_hi")
        parts_hi = sem("parts_hi")
        max_split = sem("max_split")
        gelu_hi = sem("gelu_hi")
        maskbc_loaded = sem("maskbc_loaded")
        maskt_loaded = sem("maskt_loaded")
        zeroed = sem("zeroed")
        consts_ready = sem("consts_ready")
        csum_full = sem("csum_full")
        gates_act = sem("gates_act")
        setup_done = sem("setup_done")
        var_ready = sem("var_ready")
        rs_act = sem("rs_act")
        xstat_ready = sem("xstat_ready")
        proj_full = sem("proj_full")
        qk_ready = sem("qk_ready")
        v_ready = sem("v_ready")
        wo_read = sem("wo_read")
        s_full = sem("s_full")
        max_done = sem("max_done")
        st_full = sem("st_full")
        exp_done = sem("exp_done")
        av_full = sem("av_full")
        ln_done = sem("ln_done")
        rden_done = sem("rden_done")
        o_done = sem("o_done")
        gelu_done = sem("gelu_done")
        x1_added = sem("x1_added")
        mask_ready = sem("mask_ready")
        t_full = sem("t_full")
        t_copied = sem("t_copied")
        lg_full = sem("lg_full")
        lg_copied = sem("lg_copied")
        sel_full = sem("sel_full")
        small_req = sem("small_req")
        small_done = sem("small_done")
        xp_first = sem("xp_first")
        xpre_ready = sem("xpre_ready")
        xt_full = sem("xt_full")
        xt_copied = sem("xt_copied")
        y_full = sem("y_full")
        coef_ready = sem("coef_ready")
        acc_ready = sem("acc_ready")
        out_ready = sem("out_ready")
        out_stored = [sem(f"out_stored{i}") for i in range(2)]
        dve_setup = sem("dve_setup")
        dve_att = sem("dve_att")
        dve_ffn = sem("dve_ffn")

        xr = x.rearrange("b (t p) s -> b t p s", p=P)
        cr = ctx4.rearrange("b (t p) s -> b p t s", p=P)
        outr = out.rearrange("b (t p) s -> b t p s", p=P)

        WEIGHTS = [
            *((dst.rearrange("p (t e) -> p t e", t=src.shape[0] // P), src.rearrange("(t p) e -> p t e", p=P))
              for dst, src in zip(w_raw, (wq_t, wk_t, wv_t, wo_t))),
            (wb[:], w_branch.rearrange("(t p) e -> p t e", p=P)), (wf[:], wf_t.rearrange("(t p) e -> p t e", p=P)),
            (bq_sb[:], bq), (bk_sb[:], bk), (bv_sb[:], bv), (bo_sb[:], bo), (base_sb[:], base),
            (id_sb[:], ident), (sti[:], stack_i), (eye_sb[:], eye4), (gate_sb[:], gates),
        ]

        SINK_PER_STEP = 3
        XPRE_STEPS = [16, 19, 22, 25]
        BRANCH_AT = 3
        OUT_STEPS = [[k + 4, k + 5] for k in XPRE_STEPS]
        STEPS = UNITS + 2
        T_EARLY = 2
        T_FIRST = 2

        block = ctx.enter_context(nc.Block())

        def o_part(et, w, m):
            both = o_sb[:, w % 2, et, :].bitcast(BF16)
            return both[:, m * WO_COLS:(m + 1) * WO_COLS]

        @block.sync
        def _(sp):
            for dst, src in WEIGHTS:
                sp.dma_start(dst, src).then_inc(w_loaded, 16)

            def load_x(b, t, into):
                sp.dma_start(x2[into][:, t, :], xr[bass.ds(b, 1), t].rearrange("o p s -> (o p) s")).then_inc(x_loaded[t], 16)

            def load_ctx(b, c):
                sp.dma_start(ctx_raw[:], cr[bass.ds(b, 1), :, :, c * CH:(c + 1) * CH]
                             .rearrange("o p t s -> (o p) t s")).then_inc(ctx_loaded, 16)

            def load_masks(b):
                sp.dma_start(maskbc[:], mask_bc[bass.ds(b, 1), :].broadcast_to([P, S])).then_inc(maskbc_loaded, 16)
                sp.dma_start(maskt[:], mask_t[bass.ds(b, 1)].rearrange("o p w -> (o p) w")).then_inc(maskt_loaded, 16)

            def stack(b, c, dst, blocks):
                for r, (src, part) in enumerate(blocks):
                    for h in range(HPT):
                        sp.dma_start(dst[r * DH:(r + 1) * DH, c % 2, :, h, :],
                                     src[h * DH:(h + 1) * DH, part, :, :]).then_inc(stack_loaded[c % 2], 16)

            def body(b, turn, more, first=False):
                for c in range(NC):
                    sp.wait_ge(qk_ready, b * (4 * NC) + 4 * c + 2)
                    stack(b, c, q_st, ((q_hl, 0), (q_hl, 1), (q_hl, 0)))
                    sp.wait_ge(qk_ready, b * (4 * NC) + 4 * c + 4)
                    stack(b, c, k_st, ((k_hl, 0), (k_hl, 0), (k_hl, 1)))
                    sp.wait_ge(negrow_ready, b * NC + c + 1)
                    sp.dma_start(k_st[ROWS:ROWS + 1, c % 2].rearrange("p t h j -> p (t h) j"),
                                 bcast(neg_row[:, c % 2, :], 1, HEADS)).then_inc(stack_loaded[c % 2], 16)
                    if c < NC - 2:
                        sp.wait_ge(ctx_split, b * NC + c + 2)
                        load_ctx(b, c + 2)
                    if c == NC - 2 and more:
                        sp.wait_ge(ctx_split, b * NC + NC)
                        load_ctx(b + 1, 0)
                if more:
                    for t in range(DT):
                        if not first:
                            sp.wait_ge(out_ready, (b - 1) * (2 * DT) + 2 * (t + 1))
                        load_x(b + 1, t, 1 - turn)
                    sp.wait_ge(wo_read, (b + 1) * (DT * NW))
                    load_masks(b + 1)
                    sp.wait_ge(ctx_split, (b + 1) * NC + 1)
                    load_ctx(b + 1, 1)

            load_ctx(0, 0)
            for t in range(DT):
                load_x(0, t, 0)
            load_masks(0)
            sp.wait_ge(ctx_split, 1)
            load_ctx(0, 1)
            sp.wait_ge(setup_done, 2)
            sp.wait_ge(w_split, 5)
            body(0, 0, True, first=True)
            with sp.Fori(0, B // 2 - 1) as both:
                b = 2 * both + 1
                body(b, 1, True)
                body(b + 1, 0, True)
            body(B - 1, 1, False)

        @block.gpsimd
        def _(pool):
            pool.memset(q_st[ROWS:ROWS + 1], 1.0).then_inc(zeroed, 1)
            pool.wait_ge(zeroed, 1)
            pool.memset(spare[:, 2:3], 0.0).then_inc(zeroed, 1)
            pool.wait_ge(zeroed, 2)

            def split_ctx(b, c):
                for t in range(DT):
                    pool.wait_ge(ctx_hi, b * (NC * DT) + c * DT + t + 1)
                    ins = nc.gpsimd.tensor_tensor(ctx_hl[:, 1, t, :], ctx_raw[:, t, :], ctx_hl[:, 0, t, :],
                                                  ALU.subtract)
                ins.then_inc(ctx_split, 1)

            def split_x(b, c, t, xa, first=False):
                n = c * DT + t
                if n == 0:
                    pool.wait_ge(xstat_ready, b + 1)
                    nc.gpsimd.tensor_tensor(spare[:, 4:5], spare[:, 2:3], spare[:, 2:3], ALU.add)
                nc.gpsimd.tensor_scalar(xn[:, n % 2, :], xa[:, t, c * CH:(c + 1) * CH],
                                        ra[:, 2, t:t + 1], ra[:, 4, t:t + 1], ALU.mult, ALU.add
                                        ).then_inc(x_norm, 1)
                pool.wait_ge(x_norm, b * (NC * DT) + n + 1)
                pool.wait_ge(x_hi, b * (NC * DT) + n + 1)
                if not (first and n == 0):
                    pool.wait_ge(x_split, b * (NC * DT) + n)
                nc.gpsimd.tensor_tensor(x_hl[:, 1, t, :], xn[:, n % 2, :], x_hl[:, 0, t, :], ALU.subtract
                                        ).then_inc(x_split, 1)

            def split_max(b, u, first):
                pool.wait_ge(max_done, b * UNITS + u + 1)
                if not (first and u < 2):
                    pool.wait_ge(st_full, b * UNITS + u - 1)
                nc.gpsimd.tensor_tensor(negm_hl[:, u % 2, 0, :], negm[:, u % 2, :], zero4[:], ALU.add
                                        ).then_inc(parts_hi, 1)
                pool.wait_ge(parts_hi, b * UNITS + u + 1)
                nc.gpsimd.tensor_tensor(negm_hl[:, u % 2, 1, :], negm[:, u % 2, :], negm_hl[:, u % 2, 0, :],
                                        ALU.subtract).then_inc(max_split, 1)

            def add_attention(b, w, t, xa):
                n = w * DT + t
                cols = xa[:, t, w * WO_COLS:(w + 1) * WO_COLS]
                pool.wait_ge(wo_read, b * (DT * NW) + n + 1)
                nc.gpsimd.tensor_tensor(cols, cols, wo_tmp[:, n % 2, :], ALU.add).then_inc(x1_added, 1)

            def store(bf, t, pair):
                pool.wait_ge(out_ready, bf * (2 * DT) + 2 * t + pair + 1)
                half = slice(2 * pair * C, 2 * (pair + 1) * C)
                pool.dma_start(outr[bass.ds(bf, 1), t, :, half].rearrange("o p s -> (o p) s"),
                               otile[:, 2 * pair:2 * pair + 2, :].rearrange("p n c -> p (n c)")
                               ).then_inc(out_stored[pair], 16)

            def body(b, turn, att, ffn, more=True, first=False):
                bf, xa, xb = b - 1, x2[turn], x2[1 - turn]
                if att:
                    split_ctx(b, 1)
                    for t in range(DT):
                        split_x(b, 1, t, xa)
                for k in range(STEPS):
                    if att:
                        if k < UNITS:
                            split_max(b, k, first)
                        c, r = divmod(k, UPC)
                        if c + 2 < NC:
                            if r >= 4:
                                split_x(b, c + 2, r - 4, xa)
                            if r == 6:
                                split_ctx(b, c + 2)
                        if more and c + 2 == NC and r == 7:
                            split_ctx(b + 1, 0)
                        if 0 < c < NC and r >= OUTPUT_AT:
                            for t in range(2 * (r - OUTPUT_AT), 2 * (r - OUTPUT_AT) + 2):
                                add_attention(b, c - 1, t, xa)
                    if ffn:
                        for t in range(DT):
                            for pair in range(2):
                                if k == OUT_STEPS[t][pair]:
                                    store(bf, t, pair)
                for t in range(DT):
                    if more:
                        split_x(b + 1, 0, t, xb)
                    if att:
                        add_attention(b, NC - 1, t, xa)

            split_ctx(0, 0)
            for t in range(DT):
                split_x(0, 0, t, x2[0], True)
            body(0, 0, True, False, first=True)
            with pool.Fori(0, B // 2 - 1) as both:
                b = 2 * both + 1
                body(b, 1, True, True)
                body(b + 1, 0, True, True)
            body(B - 1, 1, True, True, more=False)
            body(B, 0, False, True, more=False)
            for pair in range(2):
                pool.wait_ge(out_stored[pair], 16 * DT * B)

        @block.tensor
        def _(pe):
            def pr_free(b, n):
                if n < 2:
                    pe.wait_ge(wo_read, b * (DT * NW) - 1 + n)
                else:
                    kind, c, i = PROJ_USES[n - 2]
                    if kind == "v":
                        pe.wait_ge(v_ready, b * (2 * NC) + 2 * c + i + 1)
                    elif kind == "o":
                        pe.wait_ge(wo_read, b * (DT * NW) + c * DT + i + 1)
                    else:
                        pe.wait_ge(qk_ready, b * (4 * NC) + 4 * c + 2 * "qk".index(kind) + i + 1)

            PARTS = ((0, 0), (0, 1), (1, 0))

            def project(b, kind, c, i, first):
                n = use(kind, c, i)
                if not (first and n < 2):
                    pr_free(b, n)
                bank = pr[n % 2]
                if kind in "qk":
                    if i == 0 and kind == "q":
                        pe.wait_ge(x_split, b * (NC * DT) + (c + 1) * DT)
                    w = {"q": wq, "k": wk}[kind]
                    for t in range(DT):
                        for a, m in PARTS:
                            ins = nc.tensor.matmul(bank[:], w[:, a, t, i * P:(i + 1) * P], x_hl[:, m, t, :],
                                                   start=(t == 0 and a + m == 0), stop=(t == DT - 1 and a == 1))
                else:
                    if i == 0:
                        pe.wait_ge(ctx_split, b * NC + c + 1)
                    for j in range(2):
                        win = slice((2 * i + j) * W, (2 * i + j + 1) * W)
                        for t in range(DT):
                            for a, m in PARTS:
                                ins = nc.tensor.matmul(bank[:, j * E:(j + 1) * E], ctx_hl[:, a, t, win],
                                                       wv[:, m, t, :],
                                                       start=(t == 0 and a + m == 0), stop=(t == DT - 1 and a == 1))
                ins.then_inc(proj_full, 1)

            def place(u):
                c, r = divmod(u, UPC)
                return c, r // ET, r % ET

            def scores(b, u, first):
                c, w, et = place(u)
                if u % UPC == 0:
                    pe.wait_ge(stack_loaded[c % 2], b * (STACKED * NC // 2) + STACKED * (c // 2 + 1))
                if not (first and u == 0):
                    pe.wait_ge(max_done, b * UNITS + u)
                win = slice(w * W, (w + 1) * W)
                for h in range(HPT):
                    ins = nc.tensor.matmul(s_ps[:, h * W:(h + 1) * W], q_st[0:ROWS + 1, c % 2, et, h, win],
                                           k_st[0:ROWS + 1, c % 2, et, h, win], start=True, stop=True)
                ins.then_inc(s_full, 1)

            def scores_t(b, u, first):
                c, w, et = place(u)
                if not (first and u < 2):
                    pe.wait_ge(exp_done, b * UNITS + u - 1)
                win = slice(w * W, (w + 1) * W)
                bank = st_ps[u % 2]
                pe.wait_ge(max_split, b * UNITS + u + 1)
                for h in range(HPT):
                    part = bank[:, h * W:(h + 1) * W]
                    nc.tensor.matmul(part, k_st[0:ROWS, c % 2, et, h, win], q_st[0:ROWS, c % 2, et, h, win],
                                     start=True, stop=False)
                    for m in range(2):
                        ins = nc.tensor.matmul(part, negm_hl[:, u % 2, m, h:h + 1].broadcast_to([P, P]), id_bf[:],
                                               start=False, stop=(m == 1))
                ins.then_inc(st_full, 1)

            def values(b, u, first):
                c, w, et = place(u)
                pe.wait_ge(exp_done, b * UNITS + u + 1)
                if u % UPC == 0:
                    pe.wait_ge(v_ready, b * (2 * NC) + 2 * c + 2)
                if not (first and u == 0):
                    pe.wait_ge(o_done, b * UNITS + u)
                for h in range(HPT):
                    rows = slice(h * DH, (h + 1) * DH)
                    nc.tensor.matmul(av_ps[rows, 0:W], v_t[:, c % 2, w, et * P + h * DH:et * P + (h + 1) * DH],
                                     probs[:, u % 2, h * W:(h + 1) * W], start=True, stop=True)
                for h in range(HPT):
                    rows = slice(h * DH, (h + 1) * DH)
                    ins = nc.tensor.matmul(av_ps[rows, W:2 * W], ones[:, 0:DH],
                                           probs[:, u % 2, h * W:(h + 1) * W], start=True, stop=True)
                ins.then_inc(av_full, 1)

            def output(b, w, t):
                n = use("o", w, t)
                pr_free(b, n)
                if t == 0:
                    pe.wait_ge(gelu_done, b * (ET * NW) + ET * (w + 1))
                for et in range(ET):
                    for a, m in PARTS:
                        ins = nc.tensor.matmul(pr[n % 2][:], wo[:, a, et, t * P:(t + 1) * P], o_part(et, w, m),
                                               start=(et == 0 and a + m == 0), stop=(et == ET - 1 and a == 1))
                ins.then_inc(proj_full, 1)

            def transpose_x(bf, k, xb):
                if k % (CH // P) == 0:
                    pe.wait_ge(x1_added, bf * (DT * NW) + DT * (k // (CH // P) + 1))
                if k >= 2:
                    pe.wait_ge(t_copied, bf * SC + k - 1)
                for t in range(DT):
                    ins = nc.tensor.transpose(t_ps[k % 2][:, t * P:(t + 1) * P], xb[:, t, k * P:(k + 1) * P], id_sb[:])
                ins.then_inc(t_full, 1)

            def logits(bf, k):
                pe.wait_ge(t_copied, bf * SC + k + 1)
                g = k % 4
                nc.tensor.matmul(f1[g * NL:(g + 1) * NL, :], wf[:, k, :], xt_sb[:, k % 2, :],
                                 start=(k < 4), stop=(k >= SC - 4)).then_inc(lg_full, 1)

            def select(bf):
                pe.wait_ge(lg_copied, bf + 1)
                pe.wait_ge(t_copied, (bf + 1) * SC)
                for t in range(DT):
                    ins = nc.tensor.matmul(f0[:, t * NL:(t + 1) * NL], lgs[:, t * P:(t + 1) * P], sti[:],
                                           start=True, stop=True)
                ins.then_inc(sel_full, 1)

            def transpose_pre(bf, t):
                pe.wait_ge(xpre_ready, bf * DT + t + 1)
                if t:
                    pe.wait_ge(xt_copied, bf * DT + t)
                for j in range(C // P):
                    ins = nc.tensor.transpose(f0[:, j * P:(j + 1) * P], xpre[:, j * P:(j + 1) * P], id_sb[:])
                ins.then_inc(xt_full, 1)

            def branch(bf, t):
                pe.wait_ge(xt_copied, bf * DT + t + 1)
                if t:
                    pe.wait_ge(out_ready, bf * (2 * DT) + 2 * t)
                for j in range(C // P):
                    ins = nc.tensor.matmul(f1[:], xpt[:, j * P:(j + 1) * P], wb[:, j, :],
                                           start=(j == 0), stop=(j == C // P - 1))
                ins.then_inc(y_full, 1)

            def body(b, turn, att, ffn, first=False):
                bf, xa, xb = b - 1, x2[turn], x2[1 - turn]
                if att:
                    project(b, *FIRST_USES[0], first)
                    project(b, *FIRST_USES[1], first)
                for j in range(T_EARLY, SC):
                    if att and j == T_FIRST:
                        for i in range(2, 6):
                            project(b, *FIRST_USES[i], first)
                    if ffn:
                        transpose_x(bf, j, xb)
                        logits(bf, j - 1)
                if ffn:
                    logits(bf, SC - 1)
                    select(bf)
                for k in range(STEPS):
                    if att and k < UNITS:
                        scores(b, k, first)
                    if att:
                        if 1 <= k <= UNITS:
                            scores_t(b, k - 1, first)
                        if k >= 2:
                            values(b, k - 2, first)
                        c, r = divmod(k, UPC)
                        if c + 1 < NC and r < 6:
                            project(b, *uses_at(c)[r], first)
                        if 0 < c < NC and r >= OUTPUT_AT:
                            for t in range(2 * (r - OUTPUT_AT), 2 * (r - OUTPUT_AT) + 2):
                                output(b, c - 1, t)
                    if ffn and k - 1 in XPRE_STEPS:
                        transpose_pre(bf, XPRE_STEPS.index(k - 1))
                    if ffn and k - BRANCH_AT in XPRE_STEPS:
                        branch(bf, XPRE_STEPS.index(k - BRANCH_AT))
                if att:
                    for j in range(T_EARLY):
                        if j == 0 and not first:
                            pe.wait_ge(out_ready, (bf + 1) * (2 * DT))
                        if j == 1:
                            pe.wait_ge(max_done, (b + 1) * UNITS)
                        transpose_x(b, j, xa)
                        if j:
                            logits(b, j - 1)
                    for t in range(DT):
                        output(b, NC - 1, t)

            pe.wait_ge(w_loaded, 16 * len(WEIGHTS))
            pe.wait_ge(consts_ready, 2)
            for k in range(SC):
                ins = nc.tensor.matmul(f0[:, 0:NL], ones[:], wf[:, k, :], start=(k == 0), stop=(k == SC - 1))
            ins.then_inc(csum_full, 1)
            pe.wait_ge(setup_done, 2)
            pe.wait_ge(w_split, 5)
            pe.wait_ge(zeroed, 2)
            body(0, 0, True, False, first=True)
            with pe.Fori(0, B // 2 - 1) as both:
                b = 2 * both + 1
                body(b, 1, True, True)
                body(b + 1, 0, True, True)
            body(B - 1, 1, True, True)
            body(B, 0, False, True)

        @block.scalar
        def _(act):
            exp_k = (ke[:], zl[:], ACT.Exp, 1.0)
            ln_sum = (sln[:], ssum[:], ACT.Ln, 1.0)
            small_list = [(rb[:, 1, :], rb[:, 0, :], ACT.Ln, 1.0), (rb[:, 2, :], rb[:, 1, :], ACT.Exp, -0.5),
                          (rb[:, 1, :], rb[:, 4, :], ACT.Ln, 1.0), (rb[:, 2, :], rb[:, 1, :], ACT.Exp, -0.5),
                          (soft[:], soft[:], ACT.Exp, 1.0),
                          exp_k, ln_sum, exp_k, ln_sum, exp_k]
            a_t, v_t4 = (v[:].rearrange("p t i -> p (t i)") for v in (sa, sv))
            for _ in RETURNS:
                small_list += [(sln[:], v_t4, ACT.Ln, 1.0), (sln[:], a_t, ACT.Ln, 1.0), exp_k]
            small_at = {}
            for it in RETURNS:
                k = (it - 1) // SINK_PER_STEP
                small_at[k] = small_at.get(k, 0) + 3

            def hi_ctx(b, c, first=False):
                act.wait_ge(ctx_loaded, b * (16 * NC) + 16 * (c + 1))
                if c:
                    act.wait_ge(proj_full, b * USES + use("v", c - 1, 1) + 1)
                elif not first:
                    act.wait_ge(proj_full, (b - 1) * USES + use("v", NC - 1, 1) + 1)
                for t in range(DT):
                    nc.scalar.activation(ctx_hl[:, 0, t, :], ctx_raw[:, t, :], ACT.Copy).then_inc(ctx_hi, 1)

            def hi_x(b, c, t, xa):
                if c == 0 and t == 0:
                    act.wait_ge(xstat_ready, b + 1)
                if c and t == 0:
                    act.wait_ge(proj_full, b * USES + use("k", c - 1, 1) + 1)
                nc.scalar.activation(x_hl[:, 0, t, :], xa[:, t, c * CH:(c + 1) * CH], ACT.Identity,
                                     bias=ra[:, 4, t:t + 1], scale=ra[:, 2, t:t + 1]).then_inc(x_hi, 1)

            def xstat(b):
                act.wait_ge(var_ready, b + 1)
                nc.scalar.activation(ra[:, 1, :], ra[:, 0, :], ACT.Ln).then_inc(rs_act, 1)
                act.wait_ge(rs_act, 2 * b + 1)
                nc.scalar.activation(ra[:, 3, :], ra[:, 1, :], ACT.Exp, scale=-0.5).then_inc(rs_act, 1)

            def first_x(b, xa):
                xstat(b)
                for t in range(DT):
                    hi_x(b, 0, t, xa)

            def read_qk(b, kind, c, i, first):
                n = use(kind, c, i)
                act.wait_ge(proj_full, b * USES + n + 1)
                if i == 0 and kind == "q" and not (first and c == 0):
                    last = c - 1 if c else NC - 1
                    turns = b if c else b - 1
                    act.wait_ge(stack_loaded[last % 2], turns * (STACKED * NC // 2) + STACKED * (last // 2 + 1))
                dst, bias = {"q": (q_hl, bq_sb), "k": (k_hl, bk_sb)}[kind]
                nc.scalar.activation(dst[:, 0, i, :], pr[n % 2][:], ACT.Identity, bias=bias[:, i:i + 1]
                                     ).then_inc(qk_hi, 1)

            def read_v(b, c, i, first):
                n = use("v", c, i)
                act.wait_ge(proj_full, b * USES + n + 1)
                if i == 0 and not (first and c < 2):
                    act.wait_ge(av_full, b * UNITS + UPC * (c - 1))
                nc.scalar.activation(v_t[:, c % 2, 2 * i:2 * i + 2, :].rearrange("p w e -> p (w e)"), pr[n % 2][:],
                                     ACT.Copy).then_inc(v_ready, 1)

            def read_use(b, kind, c, i, first):
                if kind == "v":
                    read_v(b, c, i, first)
                else:
                    read_qk(b, kind, c, i, first)

            def exp_scores(b, u, first):
                g = u // ET
                act.wait_ge(st_full, b * UNITS + u + 1)
                if not (first and u < 2):
                    act.wait_ge(av_full, b * UNITS + u - 1)
                nc.scalar.activation(probs[:, u % 2, :], st_ps[u % 2][:], ACT.Exp,
                                     bias=key_bias[:, g:g + 1], scale=SCALE).then_inc(exp_done, 1)

            def inverse_den(b, u, first):
                act.wait_ge(av_full, b * UNITS + u + 1)
                if not (first and u < 2):
                    act.wait_ge(o_done, b * UNITS + u - 1)
                nc.scalar.activation(lnden[:, u % 2, :], av_ps[:, W:2 * W], ACT.Ln).then_inc(ln_done, 1)
                act.wait_ge(ln_done, b * UNITS + u + 1)
                nc.scalar.activation(rden[:, u % 2, :], lnden[:, u % 2, :], ACT.Exp, scale=-1.0
                                     ).then_inc(rden_done, 1)

            def gelu(b, c, first):
                nc.scalar.preload_act_table_set("gelu_and_others")
                act.wait_ge(o_done, b * UNITS + UPC * (c + 1))
                for et in range(ET):
                    n = c * ET + et
                    if not (first and c == 0):
                        act.wait_ge(gelu_done, b * (ET * NW) + n - 1)
                    nc.scalar.activation(g_sb[:, n % 2, :], o_sb[:, c % 2, et, :], ACT.Gelu,
                                         bias=bv_sb[:, et:et + 1]).then_inc(gelu_hi, 1)
                    act.wait_ge(gelu_hi, b * (2 * ET * NW) + 2 * n + 1)
                    nc.scalar.activation(o_part(et, c, 0), g_sb[:, n % 2, :], ACT.Copy).then_inc(gelu_hi, 1)
                nc.scalar.preload_act_table_set("natural_log_exp_and_others")

            def copy_t(bf, k):
                act.wait_ge(t_full, bf * SC + k + 1)
                if k >= 2:
                    act.wait_ge(lg_full, bf * SC + k - 1)
                nc.scalar.activation(xt_sb[:, k % 2, :], t_ps[k % 2][:], ACT.Copy).then_inc(t_copied, 1)

            def copy_lg(bf):
                act.wait_ge(lg_full, (bf + 1) * SC)
                nc.scalar.activation(lgs[:], f1[:], ACT.Copy).then_inc(lg_copied, 1)

            small = [0]

            def small_step(bf, dst, src, func, scale=1.0):
                small[0] += 1
                act.wait_ge(small_req, bf * SMALL + small[0])
                nc.scalar.activation(dst, src, func, scale=scale).then_inc(small_done, 1)

            def first_products(bf, t, xb):
                if t == 0:
                    act.wait_ge(coef_ready, 2 * bf + 1)
                else:
                    act.wait_ge(xt_full, bf * DT + t)
                nc.scalar.activation(xpre[:], xb[:, t, 0:C], ACT.Identity, bias=rb[:, 6, t:t + 1],
                                     scale=pre[:, t, 0:1]).then_inc(xp_first, 1)

            def copy_pre(bf, t):
                act.wait_ge(xt_full, bf * DT + t + 1)
                if t:
                    act.wait_ge(y_full, bf * DT + t)
                nc.scalar.activation(xpt[:], f0[:], ACT.Copy).then_inc(xt_copied, 1)

            def first_out(bf, t, pair, xb):
                if t == 0 and pair == 0:
                    act.wait_ge(coef_ready, 2 * bf + 2)
                if t:
                    act.wait_ge(out_stored[pair], 16 * (bf * DT + t))
                for i in range(2 * pair, 2 * pair + 2):
                    nc.scalar.activation(otile[:, i, :], xb[:, t, 0:C], ACT.Identity, bias=ccon[:, t, i:i + 1],
                                         scale=cmat[:, t, i, 0:1]).then_inc(acc_ready, 1)

            def small_steps(bf, n):
                for _ in range(n):
                    small_step(bf, *small_list[small[0]])

            def body(b, turn, att, ffn, more=True, first=False):
                bf, xa, xb = b - 1, x2[turn], x2[1 - turn]
                small[0] = 0
                if att:
                    read_use(b, *FIRST_USES[0], first)
                    read_use(b, *FIRST_USES[1], first)
                for j in range(T_EARLY, SC):
                    if j == T_FIRST:
                        if att:
                            for i in range(2, 6):
                                read_use(b, *FIRST_USES[i], first)
                            hi_ctx(b, 1)
                    if ffn:
                        copy_t(bf, j)
                    if ffn and j == SC - 3:
                        small_steps(bf, 4)
                    if att and 0 <= j - T_FIRST - 1 < DT:
                        hi_x(b, 1, j - T_FIRST - 1, xa)
                if ffn:
                    copy_lg(bf)
                    small_steps(bf, 6)
                for k in range(STEPS):
                    if att:
                        if 1 <= k <= UNITS:
                            exp_scores(b, k - 1, first)
                        if k >= 2:
                            inverse_den(b, k - 2, first)
                        c, r = divmod(k, UPC)
                        if c + 1 < NC and r < 6:
                            read_use(b, *uses_at(c)[r], first)
                        if c + 2 < NC:
                            if r >= 4:
                                hi_x(b, c + 2, r - 4, xa)
                            if r == 6:
                                hi_ctx(b, c + 2)
                        if more and c + 2 == NC and r == 7:
                            hi_ctx(b + 1, 0)
                        if 0 < c < NC and r == GELU_AT:
                            gelu(b, c - 1, first)
                    if ffn:
                        if k in small_at:
                            small_steps(bf, small_at[k])
                        if k + 1 in XPRE_STEPS:
                            first_products(bf, XPRE_STEPS.index(k + 1), xb)
                        if k - 1 in XPRE_STEPS:
                            copy_pre(bf, XPRE_STEPS.index(k - 1))
                        for t in range(DT):
                            for pair in range(2):
                                if k + 1 == OUT_STEPS[t][pair]:
                                    first_out(bf, t, pair, xb)
                if ffn:
                    assert small[0] == SMALL
                if att:
                    gelu(b, NC - 1, first)
                    for j in range(T_EARLY):
                        copy_t(b, j)
                if more:
                    first_x(b + 1, xb)
                if ffn:
                    for pair in range(2):
                        act.wait_ge(out_stored[pair], (bf + 1) * (16 * DT))

            act.wait_ge(w_loaded, 16 * len(WEIGHTS))
            nc.scalar.activation(gt[:, 0:2], gate_sb[:, 0:2], ACT.Tanh).then_inc(gates_act, 1)
            nc.scalar.activation(gt[:, 4:5], gate_sb[:, 2:3], ACT.Exp, scale=-1.0).then_inc(gates_act, 1)
            act.wait_ge(setup_done, 1)
            for dst, src in zip((wq, wk, wv, wo), w_raw):
                nc.scalar.activation(dst[:, 0].rearrange("p t e -> p (t e)"), src, ACT.Copy).then_inc(w_split, 1)
            nc.scalar.activation(id_bf[:], id_sb[:], ACT.Copy).then_inc(w_split, 1)
            nc.scalar.preload_act_table_set("natural_log_exp_and_others")
            hi_ctx(0, 0, True)
            first_x(0, x2[0])
            body(0, 0, True, False, first=True)
            with act.Fori(0, B // 2 - 1) as both:
                b = 2 * both + 1
                body(b, 1, True, True)
                body(b + 1, 0, True, True)
            body(B - 1, 1, True, True, more=False)
            body(B, 0, False, True, more=False)

        @block.vector
        def _(dve):
            setup = Chain(dve, dve_setup, 7)
            ca = Chain(dve, dve_att, DVE_ATT)
            cf = Chain(dve, dve_ffn, DVE_FFN)

            def newton(chain, r, guess, value, work):
                chain.link(nc.vector.tensor_tensor(work, guess, guess, ALU.mult))
                chain.link(nc.vector.tensor_tensor(work, work, value, ALU.mult))
                chain.link(nc.vector.tensor_scalar(work, work, -0.5, 1.5, ALU.mult, ALU.add))
                chain.link(nc.vector.tensor_tensor(r, guess, work, ALU.mult))

            def stat_a(b, t, xa):
                dve.wait_ge(x_loaded[t], 16 * b + 16)
                for j in range(4):
                    ins = nc.vector.bn_stats(bn_a[:, t, j, :], xa[:, t, j * 512:(j + 1) * 512])
                return ins

            def xstat(b, xa):
                ca.start(b)
                ca.link(stat_a(b, DT - 1, xa))
                nc.vector.memset(spare[:, 0:1], 0.0)
                for t in range(DT):
                    ins = nc.vector.bn_aggr(mv_a[:, t, :], bn_a[:, t].rearrange("p j s -> p (j s)"))
                ca.link(ins)
                nc.vector.tensor_scalar(ra[:, 0, :], mv_a[:, :, 1], LN_EPS, None, ALU.add).then_inc(var_ready, 1)
                dve.wait_ge(rs_act, 2 * b + 2)
                newton(ca, ra[:, 2, :], ra[:, 3, :], ra[:, 0, :], ra[:, 1, :])
                ca.end()
                nc.vector.scalar_tensor_tensor(out=ra[:, 4, :], in0=mv_a[:, :, 0], scalar=-1.0, in1=ra[:, 2, :],
                                               op0=ALU.mult, op1=ALU.mult).then_inc(xstat_ready, 1)

            def low_qk(b, kind, c, i, first):
                n = use(kind, c, i)
                m = 4 * c + 2 * "qk".index(kind) + i
                dve.wait_ge(qk_hi, b * (4 * NC) + m + 1)
                dst, bias = {"q": (q_hl, bq_sb), "k": (k_hl, bk_sb)}[kind]
                nc.vector.scalar_tensor_tensor(out=dst[:, 1, i, :], in0=pr[n % 2][:], scalar=bias[:, i:i + 1],
                                               in1=dst[:, 0, i, :], op0=ALU.add, op1=ALU.subtract
                                               ).then_inc(qk_ready, 1)
                if m == 0:
                    dve.wait_ge(maskt_loaded, 16 * b + 16)
                    nc.vector.tensor_scalar(key_bias[:], maskt[:], 0.0, NEG * SCALE, ALU.is_le, ALU.mult
                                            ).then_inc(mask_ready, 1)
                if m == 3:
                    dve.wait_ge(maskbc_loaded, 16 * b + 16)
                if m % 4 == 3:
                    nc.vector.tensor_scalar(neg_row[:, c % 2, :], maskbc[0:1, c * CH:(c + 1) * CH], 0.0, NEG,
                                            ALU.is_le, ALU.mult).then_inc(negrow_ready, 1)

            def maximum(b, u, first):
                dve.wait_ge(s_full, b * UNITS + u + 1)
                if not (first and u < 2):
                    dve.wait_ge(max_split, b * UNITS + u - 1)
                nc.vector.tensor_reduce(negm[:, u % 2, :], s_ps[:].rearrange("p (h j) -> p h j", h=HPT),
                                        AX.X, ALU.max, negate=True).then_inc(max_done, 1)

            def divide(b, u, first):
                g, et = divmod(u, ET)
                dve.wait_ge(rden_done, b * UNITS + u + 1)
                c, window = divmod(g, WPC)
                if u % UPC == 0 and not (first and c < 2):
                    last = use("o", c - 2, DT - 1) if c >= 2 else use("o", NC + c - 2, DT - 1) - USES
                    dve.wait_ge(proj_full, b * USES + last + 1)
                nc.vector.tensor_tensor(o_sb[:, c % 2, et, window * W:(window + 1) * W], av_ps[:, 0:W], rden[:, u % 2, :], ALU.mult
                                        ).then_inc(o_done, 1)

            def read_wo(b, w, t, first):
                n = w * DT + t
                dve.wait_ge(proj_full, b * USES + use("o", w, t) + 1)
                if not (first and n < 2):
                    dve.wait_ge(x1_added, b * (DT * NW) + n - 1)
                nc.vector.scalar_tensor_tensor(out=wo_tmp[:, n % 2, :], in0=pr[use("o", w, t) % 2][:],
                                               scalar=bo_sb[:, t:t + 1], in1=maskbc[:, w * WO_COLS:(w + 1) * WO_COLS],
                                               op0=ALU.add, op1=ALU.mult).then_inc(wo_read, 1)

            small = [0]

            def ask(bf, ins):
                small[0] += 1
                ins.then_inc(small_req, 1)
                dve.wait_ge(small_done, bf * SMALL + small[0])

            def stat_b(bf, t, xb):
                if t == 0:
                    dve.wait_ge(x1_added, (bf + 1) * (DT * NW))
                for j in range(4):
                    ins = nc.vector.bn_stats(bn_b[:, t, j, :], xb[:, t, j * 512:(j + 1) * 512])
                cf.link(ins)
                nc.vector.memset(spare[:, 0:1], 0.0)
                cf.link(nc.vector.bn_aggr(mv_b[:, t, :], bn_b[:, t].rearrange("p j s -> p (j s)")))

            def stat_finish(bf):
                ask(bf, nc.vector.tensor_scalar(rb[:, 0, :], mv_b[:, :, 1], LN_EPS, None, ALU.add))
                ask(bf, nc.vector.tensor_scalar(rb[:, 7, :], mv_b[:, :, 0], -1.0, None, ALU.mult))
                newton(cf, rb[:, 3, :], rb[:, 2, :], rb[:, 0, :], rb[:, 1, :])
                cf.link(nc.vector.tensor_tensor(rb[:, 4, :], rb[:, 3, :], rb[:, 3, :], ALU.mult))
                cf.link(nc.vector.tensor_tensor(rb[:, 4, :], rb[:, 4, :], mv_b[:, :, 1], ALU.mult))
                ask(bf, nc.vector.tensor_scalar(rb[:, 4, :], rb[:, 4, :], RMS_EPS, None, ALU.add))
                ask(bf, nc.vector.tensor_tensor(rb[:, 6, :], rb[:, 7, :], rb[:, 3, :], ALU.mult))
                newton(cf, rb[:, 5, :], rb[:, 2, :], rb[:, 4, :], rb[:, 1, :])
                cf.link(nc.vector.tensor_tensor(rb[:, 5, :], rb[:, 5, :], rb[:, 3, :], ALU.mult))

            l_t = sln[:].rearrange("p (t i) -> p t i", t=DT)
            kcol = ke[:].rearrange("p t i j -> p t j i")
            zcol = zl[:].rearrange("p t i j -> p t j i")
            s_t = ssum[:].rearrange("p (t i) -> p t i", t=DT)
            m_t = smx[:].rearrange("p (t i) -> p t i", t=DT)

            def over_j(v):
                return bcast(v, 3, N)

            def over_i(v):
                return bcast(v, 2, N)

            def logits_and_softmax(bf):
                dve.wait_ge(sel_full, bf + 1)
                for t in range(DT):
                    ins = nc.vector.scalar_tensor_tensor(out=logit[:, t, :], in0=csum[:], scalar=rb[:, 7, t:t + 1],
                                                         in1=f0[:, t * NL:(t + 1) * NL], op0=ALU.mult, op1=ALU.add)
                cf.link(ins)
                for t in range(DT):
                    ins = nc.vector.scalar_tensor_tensor(out=logit[:, t, :], in0=logit[:, t, :],
                                                         scalar=rb[:, 5, t:t + 1], in1=base_sb[:],
                                                         op0=ALU.mult, op1=ALU.add)
                cf.link(ins)
                lpp = logit[:, :, N * N:N * N + 2 * N].rearrange("p t (k n) -> p t k n", k=2)
                m8 = kp[:].rearrange("p t i j -> p (t i j)")[:, 0:2 * DT].rearrange("p (t k) -> p t k", t=DT)
                cf.link(nc.vector.tensor_reduce(m8, lpp, AX.X, ALU.max))
                ask(bf, nc.vector.tensor_tensor(soft[:], lpp, bcast(m8, 3, N), ALU.subtract))
                cf.link(nc.vector.tensor_reduce(m8, soft[:], AX.X, ALU.add))
                cf.link(nc.vector.reciprocal(m8, m8))
                cf.link(nc.vector.tensor_tensor(soft[:], soft[:], bcast(m8, 3, N), ALU.mult))
                nc.vector.tensor_tensor(pre[:], soft[:, :, 0, :], bcast(rb[:, 3, :], 2, N), ALU.mult
                                        ).then_inc(coef_ready, 1)
                cf.link(nc.vector.tensor_scalar(post[:], soft[:, :, 1, :], gt[:, 1:2], None, ALU.mult))

            def sinkhorn_first(bf):
                cf.link(nc.vector.tensor_scalar(zl[:].rearrange("p t i j -> p t (i j)"), logit[:, :, 0:N * N],
                                                1.0 / TAU, None, ALU.mult))
                for z, e in ((zl[:], ke[:]), (zcol, kcol)):
                    cf.link(nc.vector.tensor_reduce(m_t, z, AX.X, ALU.max))
                    ask(bf, nc.vector.tensor_tensor(z, z, bcast(m_t, 3, N), ALU.subtract))
                    ask(bf, nc.vector.tensor_reduce(s_t, e, AX.X, ALU.add))
                    less = nc.vector.tensor_tensor(z, z, bcast(l_t, 3, N), ALU.subtract)
                    if e is kcol:
                        ask(bf, less)
                    else:
                        cf.link(less)

            def sinkhorn(bf, it):
                kpc = kp[:].rearrange("p t i j -> p t j i")
                if it % SEG == 1:
                    cf.link(nc.vector.tensor_reduce(s_t, ke[:], AX.X, ALU.add))
                else:
                    cf.link(nc.vector.tensor_tensor(kp[:], ke[:], over_i(sv[:]), ALU.mult))
                    cf.link(nc.vector.tensor_reduce(s_t, kp[:], AX.X, ALU.add))
                cf.link(nc.vector.reciprocal(sa[:], s_t))
                cf.link(nc.vector.tensor_tensor(kp[:], ke[:], over_j(sa[:]), ALU.mult))
                cf.link(nc.vector.tensor_reduce(s_t, kpc, AX.X, ALU.add))
                made = nc.vector.reciprocal(sv[:], s_t)
                if it % SEG or it == ITERS - 1:
                    cf.link(made)
                else:
                    ask(bf, made)
                    ask(bf, nc.vector.tensor_tensor(zl[:], zl[:], over_i(l_t), ALU.add))
                    ask(bf, nc.vector.tensor_tensor(zl[:], zl[:], over_j(l_t), ALU.add))

            def iterate(bf, k, part):
                it = 1 + SINK_PER_STEP * k + part
                if it < ITERS:
                    sinkhorn(bf, it)
                if it == ITERS - 1:
                    coefficients(bf)

            def coefficients(bf):
                cf.link(nc.vector.tensor_tensor(kp[:], ke[:], over_j(sa[:]), ALU.mult))
                cf.link(nc.vector.tensor_tensor(kp[:], kp[:], over_i(sv[:]), ALU.mult))
                flat = kp[:].rearrange("p t i j -> p t (i j)")
                cf.link(nc.vector.tensor_scalar(flat, flat, gt[:, 2:3], None, ALU.mult))
                cf.link(nc.vector.tensor_tensor(flat, flat, bcast(eye_g[:], 1, DT), ALU.add))
                cf.link(nc.vector.tensor_scalar(flat, flat, gt[:, 1:2], None, ALU.mult))
                cf.link(nc.vector.tensor_reduce(s_t, kp[:], AX.X, ALU.add))
                cf.link(nc.vector.tensor_tensor(ccon[:], s_t, bcast(rb[:, 6, :], 2, N), ALU.mult))
                cf.link(nc.vector.tensor_tensor(flat, flat, bcast(rb[:, 3, :], 2, N * N), ALU.mult))
                nc.vector.tensor_tensor(cmat[:].rearrange("p t i j -> p t (i j)"), flat, bcast(eye_sb[:], 1, DT),
                                        ALU.add).then_inc(coef_ready, 1)
                dve.wait_ge(coef_ready, 2 * bf + 2)

            def make_xpre(bf, t, xb):
                dve.wait_ge(xp_first, bf * DT + t + 1)
                for n in range(1, N):
                    ins = nc.vector.scalar_tensor_tensor(out=xpre[:], in0=xb[:, t, n * C:(n + 1) * C],
                                                         scalar=pre[:, t, n:n + 1], in1=xpre[:],
                                                         op0=ALU.mult, op1=ALU.add)
                    if n < N - 1:
                        cf.link(ins)
                ins.then_inc(xpre_ready, 1)

            def make_out(bf, t, pair, xb):
                streams = range(2 * pair, 2 * pair + 2)
                for j in range(1, N):
                    for i in streams:
                        if j == 1:
                            dve.wait_ge(acc_ready, bf * (DT * N) + t * N + i + 1)
                        ins = nc.vector.scalar_tensor_tensor(out=otile[:, i, :], in0=xb[:, t, j * C:(j + 1) * C],
                                                             scalar=cmat[:, t, i, j:j + 1], in1=otile[:, i, :],
                                                             op0=ALU.mult, op1=ALU.add)
                    cf.link(ins)
                if pair == 0:
                    dve.wait_ge(y_full, bf * DT + t + 1)
                for i in streams:
                    ins = nc.vector.scalar_tensor_tensor(out=otile[:, i, :], in0=f1[:], scalar=post[:, t, i:i + 1],
                                                         in1=otile[:, i, :], op0=ALU.mult, op1=ALU.add)
                ins.then_inc(out_ready, 1)

            def low_gelu(b, w, et):
                n = w * ET + et
                dve.wait_ge(gelu_hi, b * (2 * ET * NW) + 2 * n + 2)
                nc.vector.tensor_tensor(o_part(et, w, 1), g_sb[:, n % 2, :], o_part(et, w, 0), ALU.subtract
                                        ).then_inc(gelu_done, 1)

            def body(b, turn, att, ffn, more=True, first=False):
                bf, xa, xb = b - 1, x2[turn], x2[1 - turn]
                small[0] = 0
                if att:
                    for i in range(2, 6):
                        low_qk(b, *FIRST_USES[i], first)
                if ffn:
                    cf.start(bf)
                    for t in range(DT):
                        stat_b(bf, t, xb)
                    stat_finish(bf)
                    logits_and_softmax(bf)
                    sinkhorn_first(bf)
                for k in range(STEPS):
                    if att and k < UNITS:
                        maximum(b, k, first)
                    if ffn:
                        iterate(bf, k, 0)
                    if att and k >= 2:
                        divide(b, k - 2, first)
                    if ffn:
                        iterate(bf, k, 1)
                        if k in XPRE_STEPS:
                            make_xpre(bf, XPRE_STEPS.index(k), xb)
                    if att:
                        c, r = divmod(k, UPC)
                        if c + 1 < NC and r < 4:
                            low_qk(b, *uses_at(c)[r], first)
                        if 0 < c < NC and r == GELU_AT:
                            for et in range(ET):
                                low_gelu(b, c - 1, et)
                        if 0 < c < NC and r >= OUTPUT_AT:
                            for t in range(2 * (r - OUTPUT_AT), 2 * (r - OUTPUT_AT) + 2):
                                read_wo(b, c - 1, t, first)
                    if ffn:
                        iterate(bf, k, 2)
                        for t in range(DT):
                            for pair in range(2):
                                if k == OUT_STEPS[t][pair]:
                                    make_out(bf, t, pair, xb)
                    if more and k >= STEPS - DT + 1:
                        stat_a(b + 1, k - (STEPS - DT + 1), xb)
                if ffn:
                    cf.end()
                if att:
                    for et in range(ET):
                        low_gelu(b, NC - 1, et)
                if more:
                    xstat(b + 1, xb)
                if att:
                    for t in range(DT):
                        read_wo(b, NC - 1, t, first)

            nc.vector.memset(ones[:], 1.0).then_inc(consts_ready, 1)
            nc.vector.memset(zero4[:], 0.0).then_inc(consts_ready, 1)
            dve.wait_ge(w_loaded, 16 * len(WEIGHTS))
            dve.wait_ge(csum_full, 1)
            setup.link(nc.vector.tensor_copy(csum[:], f0[:, 0:NL]))
            dve.wait_ge(gates_act, 2)
            setup.link(nc.vector.tensor_scalar(gt[:, 5:6], gt[:, 4:5], 1.0, None, ALU.add))
            setup.link(nc.vector.reciprocal(gt[:, 2:3], gt[:, 5:6]))
            setup.link(nc.vector.tensor_scalar(gt[:, 3:4], gt[:, 2:3], -1.0, 1.0, ALU.mult, ALU.add))
            setup.link(nc.vector.tensor_scalar(eye_g[:], eye_sb[:], gt[:, 3:4], None, ALU.mult))
            setup.link(nc.vector.tensor_scalar(w_raw[3], w_raw[3], gt[:, 0:1], None, ALU.mult))
            setup.link(nc.vector.tensor_scalar(bo_sb[:], bo_sb[:], gt[:, 0:1], None, ALU.mult))
            setup.end()
            nc.vector.memset(spare[:, 0:1], 0.0).then_inc(setup_done, 1)
            for n, (dst, src) in enumerate(zip((wq, wk, wv, wo), w_raw)):
                dve.wait_ge(w_split, n + 1)
                ins = nc.vector.tensor_tensor(dst[:, 1].rearrange("p t e -> p (t e)"), src,
                                              dst[:, 0].rearrange("p t e -> p (t e)"), ALU.subtract)
            ins.then_inc(setup_done, 1)
            for t in range(DT - 1):
                stat_a(0, t, x2[0])
            xstat(0, x2[0])
            body(0, 0, True, False, first=True)
            with dve.Fori(0, B // 2 - 1) as both:
                b = 2 * both + 1
                body(b, 1, True, True)
                body(b + 1, 0, True, True)
            body(B - 1, 1, True, True, more=False)
            body(B, 0, False, True, more=False)


_OUTS = [((B, D, S), "float32")]


def kernel(x, ctx_4096, mask_Bx1x4096_ff1, g_xattn, g_ffn, L0_xattn_Wq, L0_xattn_bq, L0_xattn_Wk, L0_xattn_bk,
           L0_xattn_Wv, L0_xattn_bv, L0_xattn_Wo, L0_xattn_bo, L0_ffn_W_res, L0_ffn_W_pre, L0_ffn_W_post,
           L0_ffn_H_res_base, L0_ffn_H_pre_base, L0_ffn_H_post_base, L0_ffn_gate, L0_ffn_W_branch):
    import numpy as np
    import concourse.bacc as _bacc
    from concourse import mybir as _mybir
    from concourse.bass_utils import run_bass_kernel_spmd as _run

    A = np.asarray

    def rows(v):
        return np.broadcast_to(A(v).reshape(1, -1), (P, A(v).size))

    mask = A(mask_Bx1x4096_ff1)[:, 0, :]
    pad = np.zeros((NL - N * N - 2 * N, S), np.float32)
    ordered = [
        A(x), A(ctx_4096), mask, mask.reshape(B, S // W, W).transpose(0, 2, 1),
        np.concatenate([rows(g_xattn), rows(g_ffn), rows(L0_ffn_gate)], axis=1),
        A(L0_xattn_Wq).T, A(L0_xattn_bq).reshape(ET, P).T, A(L0_xattn_Wk).T, A(L0_xattn_bk).reshape(ET, P).T,
        A(L0_xattn_Wv).T, A(L0_xattn_bv).reshape(ET, P).T, A(L0_xattn_Wo).T, A(L0_xattn_bo).reshape(DT, P).T,
        np.concatenate([A(L0_ffn_W_res), A(L0_ffn_W_pre), A(L0_ffn_W_post), pad], axis=0).T,
        np.concatenate([rows(L0_ffn_H_res_base), rows(L0_ffn_H_pre_base), rows(L0_ffn_H_post_base),
                        np.zeros((P, NL - N * N - 2 * N), np.float32)], axis=1),
        A(L0_ffn_W_branch), np.eye(P, dtype=np.float32), np.tile(np.eye(NL, dtype=np.float32), (4, 1)),
        rows(np.eye(N, dtype=np.float32)),
    ]
    nc = _bacc.Bacc("TRN2", target_bir_lowering=False, num_devices=1, dynamic_dma_scratch_size=4096)
    arrays, args = {}, []
    for i, a in enumerate(ordered):
        a = np.ascontiguousarray(a)
        arrays[f"in_{i}_dram"] = a
        args.append(nc.dram_tensor(f"in_{i}_dram", a.shape, _mybir.dt.from_np(a.dtype), kind="ExternalInput").ap())
    for i, (shape, dtype) in enumerate(_OUTS):
        dt = _mybir.dt.from_np(np.dtype(dtype))
        args.append(nc.dram_tensor(f"out_{i}_dram", shape, dt, kind="ExternalOutput").ap())
    program(nc, *args)
    r = _run(nc, [arrays], core_ids=[0])
    return tuple(r.results[0][f"out_{i}_dram"] for i in range(len(_OUTS)))[0]
```
